# Optimizing a Trainium2 kernel written in Bass

```python
import numpy as np
import jax
import jax.numpy as jnp

def _softmax(x, axis=-1):
    return jax.nn.softmax(x, axis=axis)

def _gelu(x):
    return jax.nn.gelu(x, approximate=True)

def _silu(x):
    return jax.nn.silu(x)

def _sigmoid(x):
    return jax.nn.sigmoid(x)

def _layernorm(x, axis=-1, eps=1e-05):
    m = jnp.mean(x, axis=axis, keepdims=True)
    v = jnp.var(x, axis=axis, keepdims=True)
    return (x - m) / jnp.sqrt(v + eps)

def _scatter_add(tgt, idx, src, axis=0):
    return tgt.at[idx].add(src)

def _segment_sum(src, seg, n):
    return jax.ops.segment_sum(src, seg, n)
kernel_name = 'mk_gnn_resnorm_d2_gnn_r8_901800'

def setup_inputs(seed: int=0):
    np.random.seed(seed)
    _w = jnp.asarray

    def _rec_inputs():
        import jax
        import jax.numpy as jnp
        _gk = jax.random.key(seed)
        x = -0.0002117 + 1 * jax.random.normal(jax.random.fold_in(_gk, 1), (6250, 512), jnp.float32)
        src = jax.random.randint(jax.random.fold_in(_gk, 2), (100000,), 0, 6250, jnp.int32)
        dst = jax.random.randint(jax.random.fold_in(_gk, 3), (100000,), 0, 6250, jnp.int32)
        _o = jnp.argsort(dst, stable=True)
        src = src[_o]
        dst = dst[_o]
        return (x, src, dst)
    x, src, dst = _rec_inputs()

    def _L0_gnn_setup():
        import jax, jax.numpy as jnp
        import numpy as np
        BN_EPS = 1e-05

        def batch_norm(h, gamma, beta):
            mu = jnp.mean(h, axis=0)
            var = jnp.var(h, axis=0)
            return (h - mu) * jax.lax.rsqrt(var + BN_EPS) * gamma + beta
        key = jax.random.key(seed)
        ks = jax.random.split(key, 6)
        N, E, dim = (6250, 200000, 512)
        hidden = dim * 2
        x = jax.random.normal(ks[0], (N, dim), dtype=jnp.float32)
        edge_index = jax.random.randint(ks[1], (2, E), 0, N, dtype=jnp.int64)
        s1 = 1.0 / np.sqrt(dim)
        s2 = 1.0 / np.sqrt(hidden)
        return {'x': x, 'edge_index': edge_index, 'eps': jnp.float32(0.0), 'W1': jax.random.uniform(ks[2], (dim, hidden), jnp.float32, -s1, s1), 'b1': jnp.zeros((hidden,), jnp.float32), 'g1': jnp.ones((hidden,), jnp.float32), 'be1': jnp.zeros((hidden,), jnp.float32), 'W2': jax.random.uniform(ks[3], (hidden, dim), jnp.float32, -s2, s2), 'b2': jnp.zeros((dim,), jnp.float32), 'g2': jnp.ones((dim,), jnp.float32), 'be2': jnp.zeros((dim,), jnp.float32)}
    _L0_gnn_all = _L0_gnn_setup()
    _L0_gnn_in = {k: v for k, v in _L0_gnn_all.items() if k in ('eps', 'W1', 'b1', 'g1', 'be1', 'W2', 'b2', 'g2', 'be2')}
    del _L0_gnn_all

    def _L1_gnn_setup():
        import jax, jax.numpy as jnp
        import numpy as np
        N_NODES = 2500
        N_EDGES = 18750
        D_IN = 512
        D_OUT = 512
        BN_EPS = 1e-05
        key = jax.random.key(seed)
        k1, k2, k3, k4 = jax.random.split(key, 4)
        x = jax.random.normal(k1, (N_NODES, D_IN), dtype=jnp.float32)
        src = jax.random.randint(k2, (N_EDGES,), 0, N_NODES, dtype=jnp.int64)
        dst = jax.random.randint(k3, (N_EDGES,), 0, N_NODES, dtype=jnp.int64)
        W = jax.random.normal(k4, (D_OUT, D_IN), dtype=jnp.float32) * (1.0 / np.sqrt(D_IN))
        b = jnp.zeros((D_OUT,), dtype=jnp.float32)
        gamma = jnp.ones((D_OUT,), dtype=jnp.float32)
        beta = jnp.zeros((D_OUT,), dtype=jnp.float32)
        return {'x': x, 'src': src, 'dst': dst, 'W': W, 'b': b, 'gamma': gamma, 'beta': beta}
    _L1_gnn_all = _L1_gnn_setup()
    _L1_gnn_in = {k: v for k, v in _L1_gnn_all.items() if k in ('W', 'b', 'gamma', 'beta')}
    del _L1_gnn_all
    return {'x': x, 'src': src, 'dst': dst, 'L0_gnn_eps': _L0_gnn_in['eps'], 'L0_gnn_W1': _L0_gnn_in['W1'], 'L0_gnn_b1': _L0_gnn_in['b1'], 'L0_gnn_g1': _L0_gnn_in['g1'], 'L0_gnn_be1': _L0_gnn_in['be1'], 'L0_gnn_W2': _L0_gnn_in['W2'], 'L0_gnn_b2': _L0_gnn_in['b2'], 'L0_gnn_g2': _L0_gnn_in['g2'], 'L0_gnn_be2': _L0_gnn_in['be2'], 'L1_gnn_W': _L1_gnn_in['W'], 'L1_gnn_b': _L1_gnn_in['b'], 'L1_gnn_gamma': _L1_gnn_in['gamma'], 'L1_gnn_beta': _L1_gnn_in['beta']}

def reference(x, src, dst, L0_gnn_eps, L0_gnn_W1, L0_gnn_b1, L0_gnn_g1, L0_gnn_be1, L0_gnn_W2, L0_gnn_b2, L0_gnn_g2, L0_gnn_be2, L1_gnn_W, L1_gnn_b, L1_gnn_gamma, L1_gnn_beta):
    import jax
    import jax.numpy as jnp

    def _L0_gnn_ref(x, edge_index, eps, W1, b1, g1, be1, W2, b2, g2, be2):
        import jax, jax.numpy as jnp
        import numpy as np
        BN_EPS = 1e-05

        def batch_norm(h, gamma, beta):
            mu = jnp.mean(h, axis=0)
            var = jnp.var(h, axis=0)
            return (h - mu) * jax.lax.rsqrt(var + BN_EPS) * gamma + beta
        N = x.shape[0]
        src, dst = (edge_index[0], edge_index[1])
        agg = jax.ops.segment_sum(x[src], dst, num_segments=N)
        h = (1.0 + eps) * x + agg
        h = jax.nn.relu(batch_norm(h @ W1 + b1, g1, be1))
        h = h @ W2 + b2
        h = jax.nn.relu(batch_norm(h, g2, be2))
        return x + h

    def _L1_gnn_ref(x, src, dst, W, b, gamma, beta):
        import jax, jax.numpy as jnp
        import numpy as np
        N_NODES = 2500
        N_EDGES = 18750
        D_IN = 512
        D_OUT = 512
        BN_EPS = 1e-05
        n = x.shape[0]
        agg = jax.ops.segment_sum(x[src], dst, num_segments=n)
        indeg = jax.ops.segment_sum(jnp.ones(dst.shape, dtype=x.dtype), dst, num_segments=n)
        h = jnp.where(indeg[:, None] > 0, agg, x)
        h = jnp.einsum('nd,od->no', h, W) + b
        h = jax.nn.relu(h)
        mean = jnp.mean(h, axis=0)
        var = jnp.var(h, axis=0)
        h = (h - mean) * jax.lax.rsqrt(var + BN_EPS) * gamma + beta
        return h
    edge_index = jnp.stack([src, dst])
    x = _layernorm(x + _L0_gnn_ref(x, edge_index, L0_gnn_eps, L0_gnn_W1, L0_gnn_b1, L0_gnn_g1, L0_gnn_be1, L0_gnn_W2, L0_gnn_b2, L0_gnn_g2, L0_gnn_be2), axis=-1)
    x = _layernorm(x + _L1_gnn_ref(x, src, dst, L1_gnn_W, L1_gnn_b, L1_gnn_gamma, L1_gnn_beta), axis=-1)
    return x

_drawn_inputs = setup_inputs


def setup_inputs(seed=0):
    import zlib

    import numpy as np

    out = dict(_drawn_inputs(seed))
    spreads = {'L0_gnn_b1': (0.0, 0.8),
     'L0_gnn_g1': (1.0, 0.2),
     'L0_gnn_be1': (0.0, 0.1),
     'L0_gnn_b2': (0.0, 0.8),
     'L0_gnn_g2': (1.0, 0.2),
     'L0_gnn_be2': (0.0, 0.1),
     'L1_gnn_b': (0.0, 0.686),
     'L1_gnn_gamma': (1.0, 0.2),
     'L1_gnn_beta': (0.0, 0.1)}
    factors = {}
    for name, (base, spread) in spreads.items():
        noise = np.random.default_rng([zlib.crc32(name.encode()), seed]).standard_normal(out[name].shape)
        drawn = base * np.exp(spread * noise) if base else spread * noise
        out[name] = jnp.asarray(drawn.astype(out[name].dtype))
    for name, factor in factors.items():
        out[name] = (out[name] * factor).astype(out[name].dtype)
    return out
```

```python
import concourse.bass as bass
from concourse import mybir
from contextlib import ExitStack

F32 = mybir.dt.float32
F32R = mybir.dt.float32r
I32 = mybir.dt.int32
ALU = mybir.AluOpType
ACT = mybir.ActivationFunctionType
AX = mybir.AxisListType
BN_EPS = 1e-05
LN_EPS = 1e-05
P = 128


class Shapes:

    def __init__(self, n, d, e, h):
        self.N, self.D, self.E, self.H = n, d, e, h
        self.NT = max(k for k in range(1, P + 1) if n % (2 * k) == 0 and (n // (2 * k)) % 2 == 1)
        self.TILES = n // self.NT
        self.PAIRS = self.TILES // 2
        self.W = 2 * self.NT
        mean = e / self.TILES
        self.CHUNKS = -int(-(mean + 3.5 * mean**0.5) // P)
        self.GROUP = self.CHUNKS * P
        self.ALL_GROUPS = -(-e // self.GROUP)
        self.EP = max(k for k in range(1, P + 1) if e % k == 0)
        self.EC = e // self.EP
        self.KD = d // P
        self.KH = h // P
        self.BLOCKS = [0, -(-self.CHUNKS // 3), -(-2 * self.CHUNKS // 3), self.CHUNKS - 1]


class PhaseSemaphores:

    def __init__(self, nc, ctx, label):
        self.nc, self.label, self.sems = nc, label, []
        ctx.callback(self.clear)

    def __call__(self, name):
        self.sems.append(self.nc.alloc_semaphore(f"{self.label}_{name}"))
        return self.sems[-1]

    def clear(self):
        self.nc.clear_and_free_semaphores(self.sems)
        self.nc.all_engine_barrier()


def setup_phase(nc, z, m):
    with ExitStack() as ctx:
        sb = lambda name, shape, dt=F32: ctx.enter_context(nc.sbuf_tensor(name, shape, dt))
        sem = PhaseSemaphores(nc, ctx, "setup")
        dst_i = sb("dst_i", [z.EP, z.EC], I32)
        next_i = sb("next_i", [z.EP, z.EC], I32)
        dst_f = sb("dst_f", [z.EP, z.EC])
        before = sb("before", [z.EP, 2, z.EC])
        counts = sb("counts", [z.EP, z.TILES + 1])
        starts = sb("starts", [1, z.TILES + 2])
        sizes = sb("sizes", [1, z.TILES])
        flags = sb("flags", [1, 4])
        fill = sb("fill", [1, 2, z.GROUP], I32)
        w1_in = sb("w1_in", [P, z.KD, z.H])
        w2_in = sb("w2_in", [P, z.KH, z.D])
        eps_in = sb("eps_in", [P, 1])
        ones_col = sb("ones_col", [P, 1])
        partition = sb("partition", [P, 1])

        copied = sem("edges_copied")
        edges_in = sem("edges_in")
        w1_loaded = sem("w1_loaded")
        w2_loaded = sem("w2_loaded")
        small_in = sem("small_in")
        filled = sem("filled")
        tables = sem("tables")
        hi_w1 = sem("hi_w1")
        hi_w2 = sem("hi_w2")
        dve_step = sem("dve_step")
        counted = sem("counted")
        summed = sem("summed")
        small = [(m.b1, m.b1_d), (m.g1, m.g1_d), (m.be1, m.be1_d), (m.b2, m.b2_d), (m.g2, m.g2_d),
                 (m.be2, m.be2_d), (m.b3, m.b3_d), (m.g3, m.g3_d), (m.be3, m.be3_d)]

        with nc.Block(name="setup") as block:

            @block.sync
            def _(sp):
                sp.wait_ge(filled, 1)
                sp.dma_start(m.src_pad[0:z.E].rearrange("(p c) -> p c", p=z.EP),
                             m.src_d.rearrange("(p c) -> p c", p=z.EP)).then_inc(copied, 16)
                sp.dma_start(m.dst_pad[0:z.E].rearrange("(p c) -> p c", p=z.EP),
                             m.dst_d.rearrange("(p c) -> p c", p=z.EP)).then_inc(copied, 16)
                sp.dma_start(m.src_pad[z.E:z.E + z.GROUP][None, :], fill[:, 0, :]).then_inc(copied, 16)
                sp.dma_start(m.dst_pad[z.E:z.E + z.GROUP][None, :], fill[:, 1, :]).then_inc(copied, 16)
                sp.dma_start(dst_i[:], m.dst_d.rearrange("(p c) -> p c", p=z.EP)).then_inc(edges_in, 16)
                sp.wait_ge(copied, 64)
                sp.dma_start(next_i[:], m.dst_pad[1:z.E + 1].rearrange("(p c) -> p c", p=z.EP)).then_inc(edges_in, 16)
                sp.wait_ge(edges_in, 32)

            @block.gpsimd
            def _(pool):
                nc.gpsimd.memset(fill[:, 0, :], 0)
                nc.gpsimd.memset(fill[:, 1, :], z.N).then_inc(filled, 1)
                nc.gpsimd.memset(ones_col[:], 1.0)
                nc.gpsimd.memset(m.zeros[:], 0.0)
                nc.gpsimd.memset(m.ones[:], 1.0)
                nc.gpsimd.memset(m.bn_eps[:], BN_EPS)
                nc.gpsimd.memset(m.ln_eps[:], LN_EPS)
                nc.gpsimd.memset(counts[:, 0:1], 0.0)
                nc.gpsimd.memset(starts[:, z.TILES:z.TILES + 1], float(z.E))
                nc.gpsimd.iota(m.column[:], [[1, P]], base=0, channel_multiplier=0,
                               allow_small_or_imprecise_dtypes=True)
                nc.gpsimd.iota(partition[:], [[0, 1]], base=0, channel_multiplier=1,
                               allow_small_or_imprecise_dtypes=True)
                nc.gpsimd.iota(m.tile_base[:], [[z.NT, z.TILES]], base=0, channel_multiplier=0,
                               allow_small_or_imprecise_dtypes=True).then_inc(tables, 1)

            @block.scalar
            def _(act):
                with nc.allow_non_contiguous_dma(reason="vectors to one value a partition"):
                    act.dma_start(w1_in[:], m.w1_d.rearrange("(k p) n -> p k n", p=P)).then_inc(w1_loaded, 16)
                    act.dma_start(w2_in[:], m.w2_d.rearrange("(k p) n -> p k n", p=P)).then_inc(w2_loaded, 16)
                    act.dma_start(eps_in[:], m.eps_d.partition_broadcast(P)).then_inc(small_in, 16)
                    for vec, dram in small:
                        act.dma_start(vec[:], dram.rearrange("(m p) -> p m", p=P)).then_inc(small_in, 16)
                act.wait_ge(w1_loaded, 16)
                nc.scalar.activation(m.w1_hi[:], w1_in[:], ACT.Copy).then_inc(hi_w1, 1)
                act.wait_ge(w2_loaded, 16)
                nc.scalar.activation(m.w2_hi[:], w2_in[:], ACT.Copy).then_inc(hi_w2, 1)
                act.wait_ge(small_in, 16 * (1 + len(small)))

            @block.vector
            def _(dve):
                step = [0]

                def link(instruction):
                    step[0] += 1
                    instruction.then_inc(dve_step, 1)
                    dve.wait_ge(dve_step, step[0])

                dve.wait_ge(tables, 1)
                link(nc.vector.tensor_scalar(m.ident[:], m.column[:], partition[:, 0:1], None, ALU.is_equal))
                nc.vector.tensor_copy(m.column_ps, m.column[:, 0:z.NT])
                dve.wait_ge(small_in, 16 * (1 + len(small)))
                link(nc.vector.tensor_scalar(eps_in[:], eps_in[:], 1.0, None, ALU.add))
                link(nc.vector.tensor_scalar(m.self_diag[:], m.ident[0:z.NT, 0:z.NT], eps_in[0:z.NT, 0:1],
                                             None, ALU.mult))
                dve.wait_ge(edges_in, 32)
                link(nc.vector.tensor_copy(dst_f[:], dst_i[:]))
                for j in range(1, z.TILES):
                    dve.wait_ge(dve_step, step[0] - (j > 1))
                    nc.vector.tensor_scalar(before[:, j % 2, :], dst_f[:], float(j * z.NT), None, ALU.is_lt, ALU.add,
                                            accum_out=counts[:, j:j + 1]).then_inc(dve_step, 1)
                    step[0] += 1
                dve.wait_ge(dve_step, step[0])
                link(nc.vector.tensor_tensor(before[:, 0, :], dst_f[:], next_i[:], ALU.is_gt))
                nc.vector.tensor_reduce(counts[:, z.TILES:z.TILES + 1], before[:, 0, :], AX.X, ALU.add).then_inc(counted, 1)
                dve.wait_ge(hi_w1, 1)
                nc.vector.tensor_tensor(m.w1_lo[:], w1_in[:], m.w1_hi[:].bitcast(F32), ALU.subtract)
                dve.wait_ge(summed, 1)
                link(nc.vector.tensor_copy(starts[:, 0:z.TILES], m.bank(7)[0:1, 0:z.TILES]))
                link(nc.vector.tensor_tensor(sizes[:], starts[:, 1:z.TILES + 1], starts[:, 0:z.TILES], ALU.subtract))
                link(nc.vector.tensor_scalar(sizes[:], sizes[:], float(z.GROUP), None, ALU.is_gt))
                link(nc.vector.tensor_reduce(flags[:, 0:1], sizes[:], AX.X, ALU.max))
                link(nc.vector.tensor_tensor(flags[:, 1:2], flags[:, 0:1], m.bank(7)[0:1, z.TILES:z.TILES + 1], ALU.add))
                link(nc.vector.tensor_scalar(flags[:, 1:2], flags[:, 1:2], 1.0, None, ALU.min))
                link(nc.vector.tensor_scalar(flags[:, 2:3], flags[:, 1:2], -1.0, 1.0, ALU.mult, ALU.add))
                nc.vector.tensor_scalar(m.control[:, 0:z.TILES], starts[:, 0:z.TILES], flags[:, 2:3], None, ALU.mult)
                nc.vector.tensor_scalar(m.control[:, z.TILES:z.TILES + 1], flags[:, 1:2],
                                        float(z.ALL_GROUPS - 1), 1.0, ALU.mult, ALU.add)
                dve.wait_ge(hi_w2, 1)
                link(nc.vector.tensor_tensor(m.w2_lo[:], w2_in[:], m.w2_hi[:].bitcast(F32), ALU.subtract))

            @block.tensor
            def _(pe):
                pe.wait_ge(tables, 1)
                pe.wait_ge(counted, 1)
                nc.tensor.matmul(m.bank(7)[0:1, 0:z.TILES + 1], ones_col[0:z.EP, :], counts[:],
                                 start=True, stop=True).then_inc(summed, 1)


def gather_phase(nc, z, m, layer):
    KM = z.KH if layer == 0 else z.KD
    HALVES = KM // 2
    w_hi, w_lo = (m.w1_hi, m.w1_lo) if layer == 0 else (m.w3_hi, m.w3_lo)
    table = m.x_d if layer == 0 else m.x1_d
    stats = m.stats1 if layer == 0 else m.stats3
    with ExitStack() as ctx:
        sb = lambda name, shape, dt=F32: ctx.enter_context(nc.sbuf_tensor(f"{name}_{layer}", shape, dt))
        sem = PhaseSemaphores(nc, ctx, f"gather{layer}")
        two = lambda name: [sem(f"{name}{h}") for h in range(2)]
        rows = sb("rows", [P, z.CHUNKS, z.D])
        select = [sb(f"select{h}", [P, z.CHUNKS, z.NT]) for h in range(2)]
        src_i = [sb(f"src_i{h}", [P, z.CHUNKS], I32) for h in range(2)]
        dst_i = [sb(f"dst_i{h}", [P, z.CHUNKS], I32) for h in range(2)]
        local = [sb(f"local{h}", [P, z.CHUNKS]) for h in range(2)]
        own = [sb(f"own{h}", [z.NT, z.D]) for h in range(2)]
        sums = [sb(f"sums{h}", [z.NT, z.D]) for h in range(2)]
        sumsT_hi = sb("sumsT_hi", [P, z.KD, z.W], F32R)
        sumsT_lo = sb("sumsT_lo", [P, z.KD, z.W], F32R)
        if layer == 0:
            hidden = sb("hidden", [P, KM, z.W])
            edge_count = [sb(f"edge_count{h}", [P, z.NT]) for h in range(2)]
        else:
            lone_diag = [sb(f"lone_diag{h}", [z.NT, z.NT]) for h in range(2)]

        index_in = two("index_in")
        local_done = two("local_done")
        select_done = two("select_done")
        gathered = [sem(f"gathered{k}") for k in range(z.CHUNKS)]
        slots_free = sem("slots_free")
        scattered = two("scattered")
        own_in = two("own_in")
        own_used = two("own_used")
        sums_done = two("sums_done")
        turned = sem("turned")
        hi_done = sem("hi_done")
        lo_done = sem("lo_done")
        product_done = sem("product_done")
        product_out = sem("product_out")
        out_done = sem("out_done")
        stats_done = sem("stats_done")
        stored = sem("stored")
        counted = two("counted")
        waited = sem("waited")
        diag_done = two("diag_done")
        lone_done = sem("lone_done")

        def agg(h):
            return m.bank(h)[0:z.NT, :]

        turn_ps = m.banks(2, 4)
        prod_ps = m.banks(4, 6)
        count_ps = m.bank(7)

        def tiles(i, h):
            return 2 * i + h

        with nc.Block(name=f"gather{layer}") as block:

            @block.sync
            def _(sp):
                groups = sp.value_load(m.control[0:1, z.TILES:z.TILES + 1], min_val=1, max_val=z.ALL_GROUPS)
                with sp.Fori(0, z.PAIRS) as i:
                    for h in range(2):
                        tile = tiles(i, h)
                        sp.wait_ge(own_used[h], i + 1)
                        sp.dma_start(own[h][:], table[bass.ds(tile * z.NT, z.NT), :]).then_inc(own_in[h], 16)
                        start = sp.value_load(m.control[0:1, bass.ds(tile, 1)], min_val=0, max_val=z.E)
                        with sp.Fori(0, groups) as g:
                            use = i * groups + g
                            sp.wait_ge(scattered[h], use + 1)
                            at = nc.s_assert_within(
                                sp.snap(start + g * z.GROUP), 0, z.E, skip_runtime_bounds_check_because=
                                "start is 0 unless there is but one group, and the groups begin before the last edge")
                            for out, edges in ((src_i[h], m.src_pad), (dst_i[h], m.dst_pad)):
                                sp.dma_start(out[:], edges[bass.ds(at, z.GROUP)].rearrange("(p c) -> p c", p=P)
                                             ).then_inc(index_in[h], 16)

            @block.gpsimd
            def _(pool):
                groups = pool.value_load(m.control[0:1, z.TILES:z.TILES + 1], min_val=1, max_val=z.ALL_GROUPS)
                with pool.Fori(0, z.PAIRS) as i:
                    for h in range(2):
                        with pool.Fori(0, groups) as g:
                            pool.wait_ge(index_in[h], 32 * (i * groups + g) + 32)
                            group = pool.snap(tiles(i, h) * groups + g)
                            for k in range(z.CHUNKS):
                                if k in z.BLOCKS:
                                    pool.wait_ge(slots_free, 3 * group + z.BLOCKS.index(k) + 1)
                                    nc.gpsimd.sem_inc(waited, 1)
                                gather = nc.gpsimd.indirect_dma_start(
                                    rows[:, k, :], None, table, bass.IndirectOffsetOnAxis(ap=src_i[h][:, k:k + 1], axis=0))
                                gather.then_inc(gathered[k], 16)

            @block.vector
            def _(dve):
                nc.vector.sem_inc(lo_done, 1)
                nc.vector.sem_inc(stats_done, 1)
                groups = dve.value_load(m.control[0:1, z.TILES:z.TILES + 1], min_val=1, max_val=z.ALL_GROUPS)
                if layer == 1:
                    nc.vector.tensor_scalar(m.lone[:], count_ps[0:z.NT, 0:z.TILES], 0.0, None,
                                            ALU.is_equal).then_inc(lone_done, 1)
                    dve.wait_ge(lone_done, 1)

                def selection(i, h):
                    tile = tiles(i, h)
                    if layer == 1:
                        dve.wait_ge(own_used[h], i + 1)
                        nc.vector.tensor_scalar(lone_diag[h][:], m.ident[0:z.NT, 0:z.NT],
                                                m.lone[:, bass.ds(tile, 1)], None, ALU.mult).then_inc(diag_done[h], 1)
                    with dve.Fori(0, groups) as g:
                        use = dve.snap(i * groups + g)
                        dve.wait_ge(index_in[h], 32 * use + 32)
                        nc.vector.tensor_scalar(local[h][:], dst_i[h][:], m.tile_base[:, bass.ds(tile, 1)], None,
                                                ALU.subtract).then_inc(local_done[h], 1)
                        dve.wait_ge(local_done[h], use + 1)
                        dve.wait_ge(scattered[h], use + 1)
                        nc.vector.tensor_tensor(
                            select[h][:], m.column_ps[:, None, :].broadcast_to([P, z.CHUNKS, z.NT]),
                            local[h][:, :, None].broadcast_to([P, z.CHUNKS, z.NT]), ALU.is_equal
                        ).then_inc(select_done[h], 1)
                        if layer == 0:
                            dve.wait_ge(select_done[h], use + 1)
                            nc.vector.tensor_reduce(edge_count[h][:], select[h][:].rearrange("p k n -> p n k"),
                                                    AX.X, ALU.add).then_inc(counted[h], 1)

                def low_part(i):
                    dve.wait_ge(product_done, HALVES * i + 1)
                    for b in range(2):
                        dve.wait_ge(hi_done, 2 * i + b + 1)
                        half = slice(b * z.KD // 2, (b + 1) * z.KD // 2)
                        nc.vector.tensor_tensor(
                            sumsT_lo[:, half, :], turn_ps[:, b, 0:z.W * z.KD // 2].rearrange("p (k n) -> p k n", n=z.W),
                            sumsT_hi[:, half, :].bitcast(F32), ALU.subtract).then_inc(lo_done, 1)

                def statistics(i):
                    for k in range(KM):
                        dve.wait_ge(out_done, KM * i + k + 1)
                        from_ = hidden[:, k, :] if layer == 0 else m.h3T[:, k, bass.ds(i * z.W, z.W)]
                        last = nc.vector.bn_stats(stats[:, k, bass.ds(i * 6, 6)], from_)
                    last.then_inc(stats_done, 1)

                selection(0, 0)
                selection(0, 1)
                with dve.Fori(1, z.PAIRS) as i:
                    selection(i, 0)
                    low_part(i - 1)
                    selection(i, 1)
                    statistics(i - 1)
                low_part(z.PAIRS - 1)
                statistics(z.PAIRS - 1)

            @block.tensor
            def _(pe):
                for h in range(2):
                    nc.tensor.sem_inc(scattered[h], 1)
                    nc.tensor.sem_inc(own_used[h], 1)
                nc.tensor.sem_inc(slots_free, 3)
                nc.tensor.sem_inc(turned, 1)
                nc.tensor.sem_inc(product_done, 1)
                groups = pe.value_load(m.control[0:1, z.TILES:z.TILES + 1], min_val=1, max_val=z.ALL_GROUPS)

                def scatter(i, h):
                    tile = tiles(i, h)
                    pe.wait_ge(own_in[h], 16 * i + 16)
                    if layer == 1:
                        pe.wait_ge(diag_done[h], i + 1)
                    pe.wait_ge(sums_done[h], i + 1)
                    nc.tensor.matmul(agg(h), m.self_diag[:] if layer == 0 else lone_diag[h][:], own[h][:],
                                     start=True, stop=False, skip_group_check=True).then_inc(own_used[h], 1)
                    if layer == 0:
                        nc.tensor.matmul(count_ps[0:z.NT, bass.ds(tile, 1)], m.zeros[:, 0:z.NT], m.ones[:],
                                         start=True, stop=False, skip_group_check=True)
                    with pe.Fori(0, groups) as g:
                        group = pe.snap(tile * groups + g)
                        pe.wait_ge(select_done[h], i * groups + g + 1)
                        for k in range(z.CHUNKS):
                            pe.wait_ge(gathered[k], 16 * group + 16)
                            last = nc.tensor.matmul(agg(h), select[h][:, k, :], rows[:, k, :], start=False,
                                                    stop=k == z.CHUNKS - 1, skip_group_check=True)
                            if k + 1 in z.BLOCKS:
                                last.then_inc(slots_free, 1)
                        if layer == 0:
                            pe.wait_ge(counted[h], i * groups + g + 1)
                            last = nc.tensor.matmul(count_ps[0:z.NT, bass.ds(tile, 1)], edge_count[h][:], m.ones[:],
                                                    start=False, stop=True, skip_group_check=True)
                        last.then_inc(scattered[h], 1)

                def turn(i):
                    pe.wait_ge(lo_done, 2 * i + 1)
                    for h in range(2):
                        pe.wait_ge(sums_done[h], i + 2)
                    for k in range(z.KD):
                        for h in range(2):
                            at = (k % (z.KD // 2)) * z.W + h * z.NT
                            last = nc.tensor.transpose(turn_ps[:, k // (z.KD // 2), at:at + z.NT],
                                                       sums[h][:, k * P:(k + 1) * P], m.ident[0:z.NT, 0:z.NT])
                    last.then_inc(turned, 1)

                def product(i):
                    pe.wait_ge(lo_done, 2 * i + 3)
                    for b in range(HALVES):
                        pe.wait_ge(product_out, HALVES * i + b + 1)
                        for o in (2 * b, 2 * b + 1):
                            out = prod_ps[:, b % 2, (o % 2) * z.W:(o % 2 + 1) * z.W]
                            parts = [(w, s, k) for k in range(z.KD)
                                     for w, s in ((w_hi, sumsT_hi), (w_hi, sumsT_lo), (w_lo, sumsT_hi))]
                            for n, (w, s, k) in enumerate(parts):
                                last = nc.tensor.matmul(out, w[:, k, o * P:(o + 1) * P], s[:, k, :], start=n == 0,
                                                        stop=n == len(parts) - 1)
                        last.then_inc(product_done, 1)

                scatter(0, 0)
                scatter(0, 1)
                with pe.Fori(1, z.PAIRS) as i:
                    scatter(i, 0)
                    turn(i - 1)
                    product(i - 1)
                    scatter(i, 1)
                turn(z.PAIRS - 1)
                product(z.PAIRS - 1)

            @block.scalar
            def _(act):
                for h in range(2):
                    nc.scalar.sem_inc(sums_done[h], 1)
                nc.scalar.sem_inc(product_out, 2)
                nc.scalar.sem_inc(stored, 16)
                groups = act.value_load(m.control[0:1, z.TILES:z.TILES + 1], min_val=1, max_val=z.ALL_GROUPS)

                def read_sums(i, h):
                    act.wait_ge(scattered[h], (i + 1) * groups + 1)
                    act.wait_ge(turned, i + 1)
                    nc.scalar.activation(sums[h][:], agg(h), ACT.Copy).then_inc(sums_done[h], 1)

                def high_part(i):
                    act.wait_ge(turned, i + 2)
                    act.wait_ge(product_done, HALVES * i + 1)
                    for b in range(2):
                        nc.scalar.activation(
                            sumsT_hi[:, b * z.KD // 2:(b + 1) * z.KD // 2, :],
                            turn_ps[:, b, 0:z.W * z.KD // 2].rearrange("p (k n) -> p k n", n=z.W),
                            ACT.Copy).then_inc(hi_done, 1)

                def read_product(i):
                    if layer == 0:
                        act.wait_ge(stored, 16 * i + 16)
                        act.wait_ge(stats_done, i + 1)
                    for b in range(HALVES):
                        act.wait_ge(product_done, HALVES * i + b + 2)
                        for o in (2 * b, 2 * b + 1):
                            from_ = prod_ps[:, b % 2, (o % 2) * z.W:(o % 2 + 1) * z.W]
                            if layer == 0:
                                nc.scalar.activation(hidden[:, o, :], from_, ACT.Identity,
                                                     bias=m.b1[:, o:o + 1]).then_inc(out_done, 1)
                            else:
                                nc.scalar.activation(m.h3T[:, o, bass.ds(i * z.W, z.W)], from_, ACT.Relu,
                                                     bias=m.b3[:, o:o + 1]).then_inc(out_done, 1)
                        act.wait_ge(out_done, KM * i + 2 * b + 2)
                        nc.scalar.sem_inc(product_out, 1)
                    if layer == 0:
                        act.dma_start(m.hidden_d[bass.ds(i * P, P), :], hidden[:].rearrange("p k n -> p (k n)")).then_inc(stored, 16)

                read_sums(0, 0)
                read_sums(0, 1)
                with act.Fori(1, z.PAIRS) as i:
                    read_sums(i, 0)
                    high_part(i - 1)
                    read_product(i - 1)
                    read_sums(i, 1)
                high_part(z.PAIRS - 1)
                read_product(z.PAIRS - 1)
                if layer == 0:
                    act.wait_ge(stored, 16 * z.PAIRS + 16)


def batch_norm_constants(nc, z, m, dve_sem, act_sem, dve, act, stats, gamma, beta, scale, bias, blocks, tmp):
    if dve is not None:
        for k in range(blocks):
            last = nc.vector.bn_aggr(tmp[:, k, 0:2], stats[:, k, :])
        last.then_inc(dve_sem, 1)
        dve.wait_ge(act_sem, 1)
        nc.vector.reciprocal(scale[:], tmp[:, :, 2]).then_inc(dve_sem, 1)
        dve.wait_ge(dve_sem, 2)
        nc.vector.tensor_tensor(scale[:], scale[:], gamma[:], ALU.mult).then_inc(dve_sem, 1)
        dve.wait_ge(dve_sem, 3)
        nc.vector.tensor_tensor(bias[:], tmp[:, :, 0], scale[:], ALU.mult).then_inc(dve_sem, 1)
        dve.wait_ge(dve_sem, 4)
        nc.vector.tensor_tensor(bias[:], beta[:], bias[:], ALU.subtract).then_inc(dve_sem, 1)
    if act is not None:
        act.wait_ge(dve_sem, 1)
        nc.scalar.activation(tmp[:, :, 2], tmp[:, :, 1], ACT.Sqrt, bias=m.bn_eps[:, 0:1]).then_inc(act_sem, 1)
        act.wait_ge(dve_sem, 5)


def hidden_phase(nc, z, m):
    with ExitStack() as ctx:
        sb = lambda name, shape, dt=F32: ctx.enter_context(nc.sbuf_tensor(name, shape, dt))
        sem = PhaseSemaphores(nc, ctx, "hidden")
        two = lambda name: [sem(f"{name}{q}") for q in range(2)]
        act_f = [sb(f"act_f{q}", [P, z.KH, z.W]) for q in range(2)]
        act_hi = [sb(f"act_hi{q}", [P, z.KH, z.W], F32R) for q in range(2)]
        act_lo = [sb(f"act_lo{q}", [P, z.KH, z.W], F32R) for q in range(2)]
        scale, bias = sb("scale1", [P, z.KH]), sb("bias1", [P, z.KH])
        tmp = sb("bn_tmp1", [P, z.KH, 3])

        loaded = two("loaded")
        rectified = two("rectified")
        hi_done = two("hi_done")
        lo_done = two("lo_done")
        product_done = two("product_done")
        out_done = two("out_done")
        product_out = two("product_out")
        bn_dve, bn_act = sem("bn_dve"), sem("bn_act")

        def out_ps(q, o):
            return m.bank(2 * q + o // 2)[:, (o % 2) * z.W:(o % 2 + 1) * z.W]

        def in_pairs(engine, first, steady, last):
            first()
            with engine.Fori(0, z.PAIRS // 2) as i:
                steady(2 * i, i, i, 0)
                steady(2 * i + 1, i, i + 1, 1)
            last()

        with nc.Block(name="hidden") as block:

            @block.sync
            def _(sp):
                def load(v, u, q):
                    sp.wait_ge(lo_done[q], u + 1)
                    sp.dma_start(act_f[q][:].rearrange("p k n -> p (k n)"),
                                 m.hidden_d[bass.ds(v * P, P), :]).then_inc(loaded[q], 16)

                with sp.Fori(0, z.PAIRS // 2) as i:
                    load(2 * i, i, 0)
                    load(2 * i + 1, i, 1)
                load(z.PAIRS - 1, z.PAIRS // 2, 0)

            @block.scalar
            def _(act):
                for q in range(2):
                    nc.scalar.sem_inc(product_out[q], 1)
                batch_norm_constants(nc, z, m, bn_dve, bn_act, None, act, m.stats1, m.g1, m.be1, scale, bias, z.KH, tmp)

                def prepare(u, q):
                    act.wait_ge(loaded[q], 16 * u + 16)
                    for k in range(z.KH):
                        last = nc.scalar.activation(act_f[q][:, k, :], act_f[q][:, k, :], ACT.Relu,
                                                    scale=scale[:, k:k + 1], bias=bias[:, k:k + 1])
                    last.then_inc(rectified[q], 1)
                    act.wait_ge(rectified[q], u + 1)
                    act.wait_ge(product_done[q], u + 1)
                    nc.scalar.activation(act_hi[q][:], act_f[q][:], ACT.Copy).then_inc(hi_done[q], 1)

                def read_out(v, u, q):
                    act.wait_ge(product_done[q], u + 2)
                    for o in range(z.KD):
                        nc.scalar.activation(m.h2T[:, o, bass.ds(v * z.W, z.W)], out_ps(q, o), ACT.Identity,
                                             bias=m.b2[:, o:o + 1]).then_inc(out_done[q], 1)
                    act.wait_ge(out_done[q], z.KD * u + z.KD)
                    nc.scalar.sem_inc(product_out[q], 1)

                def steady(v, u, next_u, q):
                    prepare(next_u if q == 0 else next_u, 1 - q)
                    read_out(v, u, q)

                in_pairs(act, lambda: prepare(0, 0), steady,
                         lambda: read_out(z.PAIRS - 1, z.PAIRS // 2, 0))

            @block.vector
            def _(dve):
                for q in range(2):
                    nc.vector.sem_inc(lo_done[q], 1)
                batch_norm_constants(nc, z, m, bn_dve, bn_act, dve, None, m.stats1, m.g1, m.be1, scale, bias, z.KH, tmp)

                def low_part(u, q):
                    dve.wait_ge(hi_done[q], u + 1)
                    nc.vector.tensor_tensor(act_lo[q][:], act_f[q][:], act_hi[q][:].bitcast(F32),
                                            ALU.subtract).then_inc(lo_done[q], 1)

                def statistics(v, u, q):
                    for o in range(z.KD):
                        dve.wait_ge(out_done[q], z.KD * u + o + 1)
                        nc.vector.bn_stats(m.stats2[:, o, bass.ds(v * 6, 6)], m.h2T[:, o, bass.ds(v * z.W, z.W)])

                def steady(v, u, next_u, q):
                    low_part(next_u, 1 - q)
                    statistics(v, u, q)

                in_pairs(dve, lambda: low_part(0, 0), steady,
                         lambda: statistics(z.PAIRS - 1, z.PAIRS // 2, 0))

            @block.tensor
            def _(pe):
                for q in range(2):
                    nc.tensor.sem_inc(product_done[q], 1)

                def product(u, q):
                    pe.wait_ge(lo_done[q], u + 2)
                    pe.wait_ge(product_out[q], u + 1)
                    for o in range(z.KD):
                        parts = [(w, s, k) for k in range(z.KH) for w, s in (
                            (m.w2_hi, act_hi[q]), (m.w2_hi, act_lo[q]), (m.w2_lo, act_hi[q]))]
                        for n, (w, s, k) in enumerate(parts):
                            last = nc.tensor.matmul(out_ps(q, o), w[:, k, o * P:(o + 1) * P], s[:, k, :],
                                                    start=n == 0, stop=n == len(parts) - 1)
                    last.then_inc(product_done[q], 1)

                with pe.Fori(0, z.PAIRS // 2) as i:
                    product(i, 0)
                    product(i, 1)
                product(z.PAIRS // 2, 0)


def rows_phase(nc, z, m, layer):
    featT, stats = (m.h2T, m.stats2) if layer == 0 else (m.h3T, m.stats3)
    gamma, beta = (m.g2, m.be2) if layer == 0 else (m.g3, m.be3)
    table, out_d = (m.x_d, m.x1_d) if layer == 0 else (m.x1_d, m.out_d)
    times = 2.0 if layer == 0 else 1.0
    with ExitStack() as ctx:
        sb = lambda name, shape, dt=F32: ctx.enter_context(nc.sbuf_tensor(f"{name}_r{layer}", shape, dt))
        sem = PhaseSemaphores(nc, ctx, f"rows{layer}")
        two = lambda name: [sem(f"{name}{h}") for h in range(2)]
        normed = sb("normed", [P, z.KD, z.W])
        own = [sb(f"own{h}", [z.NT, z.D]) for h in range(2)]
        y = [sb(f"y{h}", [z.NT, z.D]) for h in range(2)]
        done = [sb(f"done{h}", [z.NT, z.D]) for h in range(2)]
        six = [sb(f"six{h}", [z.NT, 6]) for h in range(2)]
        mean_var = [sb(f"mean_var{h}", [z.NT, 2]) for h in range(2)]
        deviation = [sb(f"deviation{h}", [z.NT, 1]) for h in range(2)]
        inverse = [sb(f"inverse{h}", [z.NT, 1]) for h in range(2)]
        scale, bias = sb("scale", [P, z.KD]), sb("bias", [P, z.KD])
        tmp = sb("bn_tmp", [P, z.KD, 3])
        if layer == 0:
            w3_in = sb("w3_in", [P, z.KD, z.D])

        own_in = two("own_in")
        normed_done = sem("normed_done")
        rows_ps_done = two("rows_ps_done")
        y_done = two("y_done")
        six_done, aggr_done = two("six_done"), two("aggr_done")
        deviation_done, inverse_done = two("deviation_done"), two("inverse_done")
        norm_done = two("norm_done")
        stored = two("stored")
        waited = sem("waited")
        bn_dve, bn_act = sem("bn_dve"), sem("bn_act")
        w3_loaded, w3_turned = sem("w3_loaded"), sem("w3_turned")
        w3_hi_done, w3_lo_done = sem("w3_hi_done"), sem("w3_lo_done")

        with nc.Block(name=f"rows{layer}") as block:

            @block.sync
            def _(sp):
                if layer == 0:
                    sp.dma_start(w3_in[:], m.w3_d.rearrange("(k p) n -> p k n", p=P)).then_inc(w3_loaded, 16)
                for h in range(2):
                    nc.sync.sem_inc(stored[h], 16)

                def load(i):
                    for h in range(2):
                        sp.wait_ge(y_done[h], i + 1)
                        sp.dma_start(own[h][:], table[bass.ds((2 * i + h) * z.NT, z.NT), :]).then_inc(own_in[h], 16)

                def store(i):
                    for h in range(2):
                        sp.wait_ge(norm_done[h], i + 1)
                        sp.dma_start(out_d[bass.ds((2 * i + h) * z.NT, z.NT), :], done[h][:]).then_inc(stored[h], 16)

                load(0)
                with sp.Fori(1, z.PAIRS) as i:
                    load(i)
                    store(i - 1)
                store(z.PAIRS - 1)
                for h in range(2):
                    sp.wait_ge(stored[h], 16 * z.PAIRS + 16)

            @block.scalar
            def _(act):
                if layer == 0:
                    for k in range(z.KD):
                        act.wait_ge(w3_turned, k + 1)
                        nc.scalar.activation(m.w3_hi[:, k, :], m.bank(2 + k), ACT.Copy).then_inc(w3_hi_done, 1)
                batch_norm_constants(nc, z, m, bn_dve, bn_act, None, act, stats, gamma, beta, scale, bias, z.KD, tmp)
                with act.Fori(0, z.PAIRS) as i:
                    for h in range(2):
                        act.wait_ge(rows_ps_done[h], i + 1)
                    for k in range(z.KD):
                        last = nc.scalar.activation(normed[:, k, :], featT[:, k, bass.ds(i * z.W, z.W)],
                                                    ACT.Relu if layer == 0 else ACT.Identity,
                                                    scale=scale[:, k:k + 1], bias=bias[:, k:k + 1])
                    last.then_inc(normed_done, 1)
                    for h in range(2):
                        act.wait_ge(aggr_done[h], i + 1)
                        nc.scalar.activation(deviation[h][:], mean_var[h][:, 1:2], ACT.Sqrt,
                                             bias=m.ln_eps[0:z.NT, 0:1]).then_inc(deviation_done[h], 1)

            @block.tensor
            def _(pe):
                for h in range(2):
                    nc.tensor.sem_inc(rows_ps_done[h], 1)
                if layer == 0:
                    pe.wait_ge(w3_loaded, 16)
                    for k in range(z.KD):
                        for o in range(z.KD):
                            last = nc.tensor.transpose(m.bank(2 + k)[:, o * P:(o + 1) * P],
                                                       w3_in[:, o, k * P:(k + 1) * P], m.ident[:])
                        last.then_inc(w3_turned, 1)
                with pe.Fori(0, z.PAIRS) as i:
                    pe.wait_ge(normed_done, i + 1)
                    for h in range(2):
                        pe.wait_ge(y_done[h], i + 1)
                        for k in range(z.KD):
                            last = nc.tensor.transpose(m.bank(h)[0:z.NT, k * P:(k + 1) * P],
                                                       normed[:, k, h * z.NT:(h + 1) * z.NT], m.ident[:])
                        last.then_inc(rows_ps_done[h], 1)

            @block.vector
            def _(dve):
                for h in range(2):
                    nc.vector.sem_inc(y_done[h], 1)
                if layer == 0:
                    for k in range(z.KD):
                        dve.wait_ge(w3_hi_done, k + 1)
                        nc.vector.tensor_tensor(m.w3_lo[:, k, :], m.bank(2 + k), m.w3_hi[:, k, :].bitcast(F32),
                                                ALU.subtract)
                batch_norm_constants(nc, z, m, bn_dve, bn_act, dve, None, stats, gamma, beta, scale, bias, z.KD, tmp)
                with dve.Fori(0, z.PAIRS) as i:
                    for h in range(2):
                        dve.wait_ge(own_in[h], 16 * i + 16)
                        dve.wait_ge(rows_ps_done[h], i + 2)
                        nc.vector.scalar_tensor_tensor(y[h][:], own[h][:], times, m.bank(h)[0:z.NT, 0:z.D],
                                                       ALU.mult, ALU.add).then_inc(y_done[h], 1)
                        dve.wait_ge(y_done[h], i + 2)
                        nc.vector.bn_stats(six[h][:], y[h][:]).then_inc(six_done[h], 1)
                        dve.wait_ge(six_done[h], i + 1)
                        nc.vector.sem_inc(waited, 1)
                        nc.vector.bn_aggr(mean_var[h][:], six[h][:]).then_inc(aggr_done[h], 1)
                    for h in range(2):
                        dve.wait_ge(deviation_done[h], i + 1)
                        nc.vector.reciprocal(inverse[h][:], deviation[h][:]).then_inc(inverse_done[h], 1)
                        dve.wait_ge(inverse_done[h], i + 1)
                        dve.wait_ge(stored[h], 16 * i + 16)
                        nc.vector.tensor_scalar(done[h][:], y[h][:], mean_var[h][:, 0:1], inverse[h][:, 0:1],
                                                ALU.subtract, ALU.mult).then_inc(norm_done[h], 1)


class Memory:
    pass


def gnn_kernel(nc, x, src, dst, eps, w1, b1, g1, be1, w2, b2, g2, be2, w3, b3, g3, be3, out):
    z = Shapes(x.shape[0], x.shape[1], src.shape[0], w1.shape[1])
    m = Memory()
    m.x_d, m.src_d, m.dst_d, m.eps_d, m.w1_d, m.w2_d, m.w3_d, m.out_d = x, src, dst, eps, w1, w2, w3, out
    m.b1_d, m.g1_d, m.be1_d, m.b2_d, m.g2_d, m.be2_d, m.b3_d, m.g3_d, m.be3_d = b1, g1, be1, b2, g2, be2, b3, g3, be3
    m.src_pad = nc.dram_tensor("src_pad", (z.E + z.GROUP,), I32, kind="Internal").ap()
    m.dst_pad = nc.dram_tensor("dst_pad", (z.E + z.GROUP,), I32, kind="Internal").ap()
    m.hidden_d = nc.dram_tensor("hidden_d", (z.PAIRS * P, z.KH * z.W), F32, kind="Internal").ap()
    m.x1_d = nc.dram_tensor("x1_d", (z.N, z.D), F32, kind="Internal").ap()
    with ExitStack() as ctx:
        def sb(name, shape, dt=F32, side="left", scope=ctx):
            return scope.enter_context(nc.sbuf_tensor(name, shape, dt, side=side))

        psum = ctx.enter_context(nc.psum_tensor("psum", [P, 8, 512], F32))
        m.bank = lambda b: psum[:, b, :]
        m.banks = lambda a, b: psum[:, a:b, :]
        m.column_ps = psum[:, 6, 0:z.NT]
        m.column, m.ident = sb("column", [P, P]), sb("ident", [P, P])
        m.self_diag, m.zeros, m.ones = sb("self_diag", [z.NT, z.NT]), sb("zeros", [P, P]), sb("ones", [P, 1])
        m.tile_base, m.lone = sb("tile_base", [P, z.TILES]), sb("lone", [z.NT, z.TILES])
        m.control = sb("control", [1, z.TILES + 1], I32)
        m.bn_eps, m.ln_eps = sb("bn_eps", [P, 1]), sb("ln_eps", [P, 1])
        m.b1, m.g1, m.be1 = (sb(n, [P, z.KH]) for n in ("b1", "g1", "be1"))
        m.b2, m.g2, m.be2, m.b3, m.g3, m.be3 = (sb(n, [P, z.KD]) for n in ("b2", "g2", "be2", "b3", "g3", "be3"))
        m.stats1 = sb("stats1", [P, z.KH, z.PAIRS * 6])
        m.stats2 = sb("stats2", [P, z.KD, z.PAIRS * 6])
        m.stats3 = sb("stats3", [P, z.KD, z.PAIRS * 6])

        with ExitStack() as second:
            m.w2_hi = sb("w2_hi", [P, z.KH, z.D], F32R, scope=second)
            m.w2_lo = sb("w2_lo", [P, z.KH, z.D], F32R, scope=second)
            with ExitStack() as first:
                m.w1_hi = sb("w1_hi", [P, z.KD, z.H], F32R, scope=first)
                m.w1_lo = sb("w1_lo", [P, z.KD, z.H], F32R, scope=first)
                setup_phase(nc, z, m)
                gather_phase(nc, z, m, 0)
            features = ExitStack()
            m.h2T = sb("h2T", [P, z.KD, z.N], side="right", scope=features)
            hidden_phase(nc, z, m)
        m.w3_hi, m.w3_lo = sb("w3_hi", [P, z.KD, z.D], F32R), sb("w3_lo", [P, z.KD, z.D], F32R)
        rows_phase(nc, z, m, 0)
        features.close()
        m.h3T = sb("h3T", [P, z.KD, z.N], side="right")
        gather_phase(nc, z, m, 1)
        rows_phase(nc, z, m, 1)


_INS = ["x", "src", "dst", "L0_gnn_eps", "L0_gnn_W1", "L0_gnn_b1", "L0_gnn_g1", "L0_gnn_be1", "L0_gnn_W2",
        "L0_gnn_b2", "L0_gnn_g2", "L0_gnn_be2", "L1_gnn_W", "L1_gnn_b", "L1_gnn_gamma", "L1_gnn_beta"]


def kernel(**inputs):
    import numpy as np
    import concourse.bacc as bacc
    from concourse.bass_utils import run_bass_kernel_spmd

    nc = bacc.Bacc("TRN2", target_bir_lowering=False, num_devices=1)
    arrays, args = {}, []
    for name in _INS:
        a = np.asarray(inputs[name])
        a = np.ascontiguousarray(a.reshape((1,)) if a.ndim == 0 else a)
        arrays[f"{name}_in"] = a
        args.append(nc.dram_tensor(f"{name}_in", a.shape, mybir.dt.from_np(a.dtype), kind="ExternalInput").ap())
    args.append(nc.dram_tensor("rows_out", arrays["x_in"].shape, F32, kind="ExternalOutput").ap())
    gnn_kernel(nc, *args)
    return run_bass_kernel_spmd(nc, [arrays], core_ids=[0]).results[0]["rows_out"]
```

```python
import concourse.bass as bass
from concourse import mybir
from contextlib import ExitStack

F32 = mybir.dt.float32
F32R = mybir.dt.float32r
BF16 = mybir.dt.bfloat16
I32 = mybir.dt.int32
ALU = mybir.AluOpType
ACT = mybir.ActivationFunctionType
AX = mybir.AxisListType
BN_EPS = 1e-05
LN_EPS = 1e-05
P = 128
W3_BANK = 5


class Shapes:

    def __init__(self, n, d, e, h):
        self.N, self.D, self.E, self.H = n, d, e, h
        self.NT = max(k for k in range(1, P + 1) if n % (2 * k) == 0 and (n // (2 * k)) % 2 == 1)
        self.TILES = n // self.NT
        self.PAIRS = self.TILES // 2
        self.W = 2 * self.NT
        self.STEP_TILES = max(k for k in range(1, 6) if self.TILES % k == 0)
        mean = e / self.TILES
        self.CHUNKS = -int(-(mean + 3.5 * mean**0.5) // P)
        self.GROUP = self.CHUNKS * P
        self.ALL_GROUPS = -(-e // self.GROUP)
        self.SPLIT = (self.CHUNKS * 6 // 17, max(1, self.CHUNKS * 2 // 17))
        self.SLOT_BLOCKS = 4
        self.EP = max(k for k in range(1, P + 1) if e % k == 0)
        self.EC = e // self.EP
        self.KD = d // P
        self.KH = h // P

    def blocks(self, layer):
        first, whole = self.SPLIT[layer], self.CHUNKS - self.SPLIT[layer]
        return [first + -(-whole * b // self.SLOT_BLOCKS) for b in range(self.SLOT_BLOCKS)]

    def order(self, layer):
        split, whole = list(range(self.SPLIT[layer])), list(range(self.SPLIT[layer], self.CHUNKS))
        order = whole[:2]
        for n, k in enumerate(whole[2:]):
            order += split[n:n + 1] + [k]
        return order


def sprayed(count):
    most = count // 16 * 16
    return [part for part in ((0, most), (most, count)) if part[0] < part[1]]


class PhaseSemaphores:

    def __init__(self, nc, ctx, label):
        self.nc, self.label, self.sems = nc, label, []
        ctx.callback(self.clear)

    def __call__(self, name):
        self.sems.append(self.nc.alloc_semaphore(f"{self.label}_{name}"))
        return self.sems[-1]

    def clear(self):
        self.nc.clear_and_free_semaphores(self.sems)
        self.nc.all_engine_barrier()


def setup_phase(nc, z, m):
    with ExitStack() as ctx:
        sb = lambda name, shape, dt=F32: ctx.enter_context(nc.sbuf_tensor(name, shape, dt))
        sem = PhaseSemaphores(nc, ctx, "setup")
        dst_i = sb("dst_i", [z.EP, z.EC], I32)
        next_i = sb("next_i", [z.EP, z.EC], I32)
        dst_f = sb("dst_f", [z.EP, z.EC])
        side = sb("side", [z.EP, 2, z.EC])
        threshold = sb("threshold", [P, z.TILES])
        before = sb("before", [z.EP, 2, z.EC])
        counts = sb("counts", [z.EP, z.TILES + 1])
        starts = sb("starts", [1, z.TILES + 2])
        sizes = sb("sizes", [1, z.TILES])
        flags = sb("flags", [1, 4])
        fill = sb("fill", [1, 2, z.GROUP], I32)
        w1_in = sb("w1_in", [P, z.KD, z.H])
        w2_in = sb("w2_in", [P, z.KH, z.D])
        eps_in = sb("eps_in", [P, 1])
        ones_col = sb("ones_col", [P, 1])
        partition = sb("partition", [P, 1])

        copied = sem("edges_copied")
        edges_in = sem("edges_in")
        w1_loaded = sem("w1_loaded")
        w2_loaded = sem("w2_loaded")
        small_in = sem("small_in")
        filled = sem("filled")
        thresholds_done = sem("thresholds_done")
        signs = sem("signs")
        tables = sem("tables")
        hi_w1 = sem("hi_w1")
        hi_w2 = sem("hi_w2")
        dve_step = sem("dve_step")
        counted = sem("counted")
        summed = sem("summed")
        FIRST_ACT = 1 + (z.TILES - 1) * 5 // 9
        DVE_TILES, ACT_TILES = range(1, FIRST_ACT), range(FIRST_ACT, z.TILES)
        EDGE_PARTS = 16 * (len(sprayed(z.EP)) + len(sprayed(z.EP - 1)) + 2)
        small = [(m.b1, m.b1_d), (m.g1, m.g1_d), (m.be1, m.be1_d), (m.b2, m.b2_d), (m.g2, m.g2_d),
                 (m.be2, m.be2_d), (m.b3, m.b3_d), (m.g3, m.g3_d), (m.be3, m.be3_d)]

        with nc.Block(name="setup") as block:

            @block.sync
            def _(sp):
                edges = m.dst_d.rearrange("(p c) -> p c", p=z.EP)
                for a, b in sprayed(z.EP):
                    sp.dma_start(dst_i[a:b, :], edges[a:b, :]).then_inc(edges_in, 16)
                full = (z.EP - 1) * z.EC
                after = m.dst_d[1:full + 1].rearrange("(p c) -> p c", p=z.EP - 1)
                sp.wait_ge(filled, 1)
                for a, b in sprayed(z.EP - 1):
                    sp.dma_start(next_i[a:b, :], after[a:b, :]).then_inc(edges_in, 16)
                sp.dma_start(next_i[z.EP - 1:z.EP, 0:z.EC - 1], m.dst_d[full + 1:z.E][None, :]).then_inc(edges_in, 16)
                sp.dma_start(next_i[z.EP - 1:z.EP, z.EC - 1:z.EC], fill[:, 1, 0:1]).then_inc(edges_in, 16)
                for pad, edges, f in ((m.src_pad, m.src_d, 0), (m.dst_pad, m.dst_d, 1)):
                    sp.dma_start(pad[0:z.E].rearrange("(p c) -> p c", p=16), edges.rearrange("(p c) -> p c", p=16)
                                 ).then_inc(copied, 16)
                    sp.dma_start(pad[z.E:z.E + z.GROUP][None, :], fill[:, f, :]).then_inc(copied, 16)
                sp.wait_ge(copied, 64)

            @block.gpsimd
            def _(pool):
                nc.gpsimd.memset(fill[:, 0, :], 0)
                nc.gpsimd.memset(fill[:, 1, :], z.N).then_inc(filled, 1)
                nc.gpsimd.memset(ones_col[:], 1.0)
                nc.gpsimd.memset(m.zeros[:], 0.0)
                nc.gpsimd.memset(m.ones[:], 1.0)
                nc.gpsimd.memset(m.bn_eps[:], BN_EPS)
                nc.gpsimd.memset(m.ln_eps[:], LN_EPS)
                nc.gpsimd.memset(counts[:, 0:1], 0.0)
                nc.gpsimd.memset(starts[:, z.TILES:z.TILES + 1], float(z.E))
                nc.gpsimd.iota(m.column[:], [[1, P]], base=0, channel_multiplier=0,
                               allow_small_or_imprecise_dtypes=True)
                nc.gpsimd.iota(partition[:], [[0, 1]], base=0, channel_multiplier=1,
                               allow_small_or_imprecise_dtypes=True)
                nc.gpsimd.iota(m.tile_base[:], [[z.NT, z.TILES]], base=0, channel_multiplier=0,
                               allow_small_or_imprecise_dtypes=True).then_inc(tables, 1)

            @block.scalar
            def _(act):
                with nc.allow_non_contiguous_dma(reason="vectors to one value a partition"):
                    act.dma_start(eps_in[:], m.eps_d.partition_broadcast(P)).then_inc(small_in, 16)
                    act.dma_start(w1_in[:], m.w1_d.rearrange("(k p) n -> p k n", p=P)).then_inc(w1_loaded, 16)
                    act.dma_start(w2_in[:], m.w2_d.rearrange("(k p) n -> p k n", p=P)).then_inc(w2_loaded, 16)
                    for vec, dram in small:
                        act.dma_start(vec[:], dram.rearrange("(m p) -> p m", p=P)).then_inc(small_in, 16)
                act.wait_ge(w1_loaded, 16)
                nc.scalar.activation(m.w1_hi[:], w1_in[:], ACT.Copy).then_inc(hi_w1, 1)
                act.wait_ge(thresholds_done, 1)
                act.wait_ge(edges_in, EDGE_PARTS)
                for n, j in enumerate(ACT_TILES):
                    if n >= 2:
                        act.wait_ge(signs, n - 1)
                    nc.scalar.activation(side[:, n % 2, :], dst_i[:], ACT.Sign, bias=threshold[0:z.EP, j:j + 1],
                                         accum_out=counts[:, j:j + 1]).then_inc(signs, 1)
                act.wait_ge(w2_loaded, 16)
                nc.scalar.activation(m.w2_hi[:], w2_in[:], ACT.Copy).then_inc(hi_w2, 1)
                act.wait_ge(small_in, 16 * (1 + len(small)))

            @block.vector
            def _(dve):
                step = [0]

                def link(instruction):
                    step[0] += 1
                    instruction.then_inc(dve_step, 1)
                    dve.wait_ge(dve_step, step[0])

                dve.wait_ge(tables, 1)
                nc.vector.tensor_scalar(threshold[:], m.tile_base[:], -1.0, 0.5, ALU.mult,
                                        ALU.add).then_inc(thresholds_done, 1)
                link(nc.vector.tensor_scalar(m.ident[:], m.column[:], partition[:, 0:1], None, ALU.is_equal))
                nc.vector.tensor_copy(m.column_ps, m.column[:, 0:z.NT])
                dve.wait_ge(edges_in, EDGE_PARTS)
                link(nc.vector.tensor_copy(dst_f[:], dst_i[:]))
                for j in DVE_TILES:
                    dve.wait_ge(dve_step, step[0] - (j > DVE_TILES[0]))
                    nc.vector.tensor_scalar(before[:, j % 2, :], dst_f[:], float(j * z.NT), None, ALU.is_lt, ALU.add,
                                            accum_out=counts[:, j:j + 1]).then_inc(dve_step, 1)
                    step[0] += 1
                dve.wait_ge(dve_step, step[0])
                link(nc.vector.tensor_tensor(before[:, 0, :], dst_f[:], next_i[:], ALU.is_gt))
                nc.vector.tensor_reduce(counts[:, z.TILES:z.TILES + 1], before[:, 0, :], AX.X, ALU.add).then_inc(counted, 1)
                dve.wait_ge(summed, 1)
                nc.vector.tensor_scalar(starts[:, FIRST_ACT:z.TILES], m.bank(7)[0:1, FIRST_ACT:z.TILES], -0.5,
                                        0.5 * z.E, ALU.mult, ALU.add)
                link(nc.vector.tensor_copy(starts[:, 0:FIRST_ACT], m.bank(7)[0:1, 0:FIRST_ACT]))
                link(nc.vector.tensor_tensor(sizes[:], starts[:, 1:z.TILES + 1], starts[:, 0:z.TILES], ALU.subtract))
                link(nc.vector.tensor_scalar(sizes[:], sizes[:], float(z.GROUP), None, ALU.is_gt))
                link(nc.vector.tensor_reduce(flags[:, 0:1], sizes[:], AX.X, ALU.max))
                link(nc.vector.tensor_tensor(flags[:, 1:2], flags[:, 0:1], m.bank(7)[0:1, z.TILES:z.TILES + 1], ALU.add))
                link(nc.vector.tensor_scalar(flags[:, 1:2], flags[:, 1:2], 1.0, None, ALU.min))
                link(nc.vector.tensor_scalar(flags[:, 2:3], flags[:, 1:2], -1.0, 1.0, ALU.mult, ALU.add))
                nc.vector.tensor_scalar(m.control[:, 0:z.TILES], starts[:, 0:z.TILES], flags[:, 2:3], None, ALU.mult)
                nc.vector.tensor_scalar(m.control[:, z.TILES:z.TILES + 1], flags[:, 1:2],
                                        float(z.ALL_GROUPS - 1), 1.0, ALU.mult, ALU.add)
                dve.wait_ge(small_in, 16 * (1 + len(small)))
                nc.vector.tensor_scalar(m.self_weight[:], eps_in[:], 1.0, None, ALU.add)
                dve.wait_ge(hi_w1, 1)
                nc.vector.tensor_tensor(m.w1_lo[:], w1_in[:], m.w1_hi[:].bitcast(F32), ALU.subtract)
                dve.wait_ge(hi_w2, 1)
                link(nc.vector.tensor_tensor(m.w2_lo[:], w2_in[:], m.w2_hi[:].bitcast(F32), ALU.subtract))

            @block.tensor
            def _(pe):
                pe.wait_ge(tables, 1)
                pe.wait_ge(counted, 1)
                pe.wait_ge(signs, len(ACT_TILES))
                nc.tensor.matmul(m.bank(7)[0:1, 0:z.TILES + 1], ones_col[0:z.EP, :], counts[:],
                                 start=True, stop=True).then_inc(summed, 1)


def gather_phase(nc, z, m, layer):
    KM = z.KH if layer == 0 else z.KD
    OWN_PARTS = 16 * len(sprayed(z.NT))
    SPLIT = z.SPLIT[layer]
    BLOCKS = z.blocks(layer)
    HALVES = KM // 2
    w_hi, w_lo = (m.w1_hi, m.w1_lo) if layer == 0 else (m.w3_hi, m.w3_lo)
    table = m.x_d if layer == 0 else m.x1_d
    stats = m.stats1 if layer == 0 else m.stats3
    with ExitStack() as ctx:
        sb = lambda name, shape, dt=F32: ctx.enter_context(nc.sbuf_tensor(f"{name}_{layer}", shape, dt))
        sem = PhaseSemaphores(nc, ctx, f"gather{layer}")
        two = lambda name: [sem(f"{name}{h}") for h in range(2)]
        rows = sb("rows", [P, z.CHUNKS, z.D])
        rows_hi, rows_lo = sb("rows_hi", [P, SPLIT, z.D], F32R), sb("rows_lo", [P, SPLIT, z.D], F32R)
        select = [sb(f"select{h}", [P, z.CHUNKS - SPLIT, z.NT]) for h in range(2)]
        select_r = [sb(f"select_r{h}", [P, SPLIT, z.NT], F32R) for h in range(2)]
        src_i = [sb(f"src_i{h}", [P, z.CHUNKS], I32) for h in range(2)]
        dst_i = [sb(f"dst_i{h}", [P, z.CHUNKS], I32) for h in range(2)]
        local = [sb(f"local{h}", [P, z.CHUNKS]) for h in range(2)]
        own = [sb(f"own{h}", [z.NT, z.D]) for h in range(2)]
        sums = [sb(f"sums{h}", [z.NT, z.D]) for h in range(2)]
        sumsT_hi = sb("sumsT_hi", [P, z.KD, z.W], F32R)
        sumsT_lo = sb("sumsT_lo", [P, z.KD, z.W], F32R)
        if layer == 0:
            hidden = sb("hidden", [P, KM, z.W])
            edge_count = [sb(f"edge_count{h}", [P, 2, z.NT], BF16) for h in range(2)]

        index_in = two("index_in")
        local_done = two("local_done")
        select_done = two("select_done")
        gathered = [sem(f"gathered{k}") for k in range(z.CHUNKS)]
        split_hi = sem("split_hi")
        split_lo = sem("split_lo")
        split_used = sem("split_used")
        slots_free = sem("slots_free")
        scattered = two("scattered")
        own_in = two("own_in")
        sums_done = two("sums_done")
        turned = sem("turned")
        hi_done = sem("hi_done")
        lo_done = sem("lo_done")
        product_done = sem("product_done")
        product_out = sem("product_out")
        out_done = sem("out_done")
        stats_done = sem("stats_done")
        stored = sem("stored")
        counted = two("counted")
        waited = sem("waited")
        lone_done = sem("lone_done")

        def agg(h):
            return m.bank(h)[0:z.NT, :]

        turn_ps = m.banks(2, 4)
        prod_ps = m.banks(4, 6)
        count_ps = m.bank(7)

        def tiles(i, h):
            return 2 * i + h

        with nc.Block(name=f"gather{layer}") as block:

            @block.sync
            def _(sp):
                groups = sp.value_load(m.control[0:1, z.TILES:z.TILES + 1], min_val=1, max_val=z.ALL_GROUPS)
                with sp.Fori(0, z.PAIRS) as i:
                    for h in range(2):
                        tile = tiles(i, h)
                        start = sp.value_load(m.control[0:1, bass.ds(tile, 1)], min_val=0, max_val=z.E)
                        with sp.Fori(0, groups) as g:
                            use = i * groups + g
                            sp.wait_ge(scattered[h], use + 1)
                            at = nc.s_assert_within(
                                sp.snap(start + g * z.GROUP), 0, z.E, skip_runtime_bounds_check_because=
                                "start is 0 unless there is but one group, and the groups begin before the last edge")
                            for out, edges in ((src_i[h], m.src_pad), (dst_i[h], m.dst_pad)):
                                sp.dma_start(out[:], edges[bass.ds(at, z.GROUP)].rearrange("(p c) -> p c", p=P)
                                             ).then_inc(index_in[h], 16)
                        sp.wait_ge(sums_done[h], i + 1)
                        for a, b in sprayed(z.NT):
                            sp.dma_start(own[h][a:b, :], table[bass.ds(tile * z.NT + a, b - a), :]).then_inc(own_in[h], 16)

            @block.gpsimd
            def _(pool):
                groups = pool.value_load(m.control[0:1, z.TILES:z.TILES + 1], min_val=1, max_val=z.ALL_GROUPS)
                with pool.Fori(0, z.PAIRS) as i:
                    for h in range(2):
                        with pool.Fori(0, groups) as g:
                            pool.wait_ge(index_in[h], 32 * (i * groups + g) + 32)
                            group = pool.snap(tiles(i, h) * groups + g)
                            for k in range(z.CHUNKS):
                                if k == 0 and SPLIT:
                                    pool.wait_ge(split_lo, SPLIT * group + SPLIT)
                                    nc.gpsimd.sem_inc(waited, 1)
                                elif k in BLOCKS:
                                    pool.wait_ge(slots_free, z.SLOT_BLOCKS * group + BLOCKS.index(k) + 1)
                                    nc.gpsimd.sem_inc(waited, 1)
                                gather = nc.gpsimd.indirect_dma_start(
                                    rows[:, k, :], None, table, bass.IndirectOffsetOnAxis(ap=src_i[h][:, k:k + 1], axis=0))
                                gather.then_inc(gathered[k], 16)

            @block.vector
            def _(dve):
                nc.vector.sem_inc(lo_done, 1)
                nc.vector.sem_inc(split_lo, SPLIT)
                nc.vector.sem_inc(stats_done, 1)
                for h in range(2):
                    nc.vector.sem_inc(sums_done[h], 1)
                groups = dve.value_load(m.control[0:1, z.TILES:z.TILES + 1], min_val=1, max_val=z.ALL_GROUPS)
                if layer == 1:
                    nc.vector.tensor_scalar(m.lone[:], count_ps[0:z.NT, 0:z.TILES], 0.0, None,
                                            ALU.is_equal).then_inc(lone_done, 1)
                    dve.wait_ge(lone_done, 1)

                def selection(i, h):
                    tile = tiles(i, h)
                    with dve.Fori(0, groups) as g:
                        use = dve.snap(i * groups + g)
                        dve.wait_ge(index_in[h], 32 * use + 32)
                        nc.vector.tensor_scalar(local[h][:], dst_i[h][:], m.tile_base[:, bass.ds(tile, 1)], None,
                                                ALU.subtract).then_inc(local_done[h], 1)
                        dve.wait_ge(local_done[h], use + 1)
                        dve.wait_ge(scattered[h], use + 1)
                        for out, a, b in ((select_r[h], 0, SPLIT), (select[h], SPLIT, z.CHUNKS)):
                            nc.vector.tensor_tensor(
                                out[:], m.column_ps[:, None, :].broadcast_to([P, b - a, z.NT]),
                                local[h][:, a:b, None].broadcast_to([P, b - a, z.NT]), ALU.is_equal
                            ).then_inc(select_done[h], 1)
                        group = dve.snap(tile * groups + g)
                        for k in range(SPLIT):
                            dve.wait_ge(split_hi, group * SPLIT + k + 1)
                            nc.vector.tensor_tensor(rows_lo[:, k, :], rows[:, k, :], rows_hi[:, k, :].bitcast(F32),
                                                    ALU.subtract).then_inc(split_lo, 1)
                        if layer == 0:
                            dve.wait_ge(select_done[h], 2 * use + 2)
                            with nc.allow_low_precision(reason="counts up to CHUNKS are exact in bfloat16"):
                                nc.vector.tensor_reduce(edge_count[h][:, 0, :],
                                                        select_r[h][:].bitcast(F32).rearrange("p k n -> p n k"),
                                                        AX.X, ALU.add)
                                nc.vector.tensor_reduce(edge_count[h][:, 1, :], select[h][:].rearrange("p k n -> p n k"),
                                                        AX.X, ALU.add).then_inc(counted[h], 1)

                def read_sums(i, h):
                    dve.wait_ge(own_in[h], OWN_PARTS * (i + 1))
                    dve.wait_ge(scattered[h], (i + 1) * groups + 1)
                    dve.wait_ge(turned, i + 1)
                    weight = m.self_weight[0:z.NT, :] if layer == 0 else m.lone[:, bass.ds(tiles(i, h), 1)]
                    nc.vector.scalar_tensor_tensor(sums[h][:], own[h][:], weight, agg(h), ALU.mult,
                                                   ALU.add).then_inc(sums_done[h], 1)

                def low_part(i):
                    dve.wait_ge(product_done, HALVES * i + 1)
                    for b in range(2):
                        dve.wait_ge(hi_done, 2 * i + b + 1)
                        half = slice(b * z.KD // 2, (b + 1) * z.KD // 2)
                        nc.vector.tensor_tensor(
                            sumsT_lo[:, half, :], turn_ps[:, b, 0:z.W * z.KD // 2].rearrange("p (k n) -> p k n", n=z.W),
                            sumsT_hi[:, half, :].bitcast(F32), ALU.subtract).then_inc(lo_done, 1)

                def statistics(i):
                    for k in range(KM):
                        dve.wait_ge(out_done, KM * i + k + 1)
                        from_ = hidden[:, k, :] if layer == 0 else m.h3T[:, k, bass.ds(i * z.W, z.W)]
                        last = nc.vector.bn_stats(stats[:, k, bass.ds(i * 6, 6)], from_)
                    last.then_inc(stats_done, 1)

                selection(0, 0)
                selection(0, 1)
                read_sums(0, 0)
                read_sums(0, 1)
                selection(1, 0)
                with dve.Fori(1, z.PAIRS - 1) as i:
                    selection(i, 1)
                    read_sums(i, 0)
                    low_part(i - 1)
                    read_sums(i, 1)
                    selection(i + 1, 0)
                    statistics(i - 1)
                selection(z.PAIRS - 1, 1)
                read_sums(z.PAIRS - 1, 0)
                low_part(z.PAIRS - 2)
                read_sums(z.PAIRS - 1, 1)
                statistics(z.PAIRS - 2)
                low_part(z.PAIRS - 1)
                statistics(z.PAIRS - 1)

            @block.tensor
            def _(pe):
                for h in range(2):
                    nc.tensor.sem_inc(scattered[h], 1)
                nc.tensor.sem_inc(slots_free, z.SLOT_BLOCKS)
                nc.tensor.sem_inc(split_used, 1)
                nc.tensor.sem_inc(turned, 1)
                nc.tensor.sem_inc(product_done, 1)
                groups = pe.value_load(m.control[0:1, z.TILES:z.TILES + 1], min_val=1, max_val=z.ALL_GROUPS)

                def scatter(i, h):
                    tile = tiles(i, h)
                    pe.wait_ge(sums_done[h], i + 1)
                    nc.tensor.matmul(agg(h)[:, 0:1], m.zeros[:, 0:z.NT], m.ones[:, 0:1],
                                     start=True, stop=False, skip_group_check=True)
                    with pe.Fori(0, groups) as g:
                        group = pe.snap(tile * groups + g)
                        pe.wait_ge(select_done[h], 2 * (i * groups + g) + 2)
                        for k in z.order(layer):
                            if k < SPLIT:
                                pe.wait_ge(split_lo, (group + 1) * SPLIT + k + 1)
                                nc.tensor.matmul(agg(h), select_r[h][:, k, :], rows_hi[:, k, :], start=False,
                                                 stop=False, skip_group_check=True)
                                last = nc.tensor.matmul(agg(h), select_r[h][:, k, :], rows_lo[:, k, :], start=False,
                                                        stop=False, skip_group_check=True)
                            else:
                                pe.wait_ge(gathered[k], 16 * group + 16)
                                last = nc.tensor.matmul(agg(h), select[h][:, k - SPLIT, :], rows[:, k, :], start=False,
                                                        stop=layer == 0 and k == z.CHUNKS - 1, skip_group_check=True)
                            if k == SPLIT - 1:
                                last.then_inc(split_used, 1)
                            if k >= SPLIT and (k + 1 in BLOCKS or k + 1 == z.CHUNKS):
                                last.then_inc(slots_free, 1)
                        if layer == 0:
                            pe.wait_ge(counted[h], i * groups + g + 1)
                            for n in range(2):
                                last = nc.tensor.matmul(count_ps[0:z.NT, bass.ds(tile, 1)], edge_count[h][:, n, :],
                                                        m.ones[:, 0:1], start=False, stop=n == 1,
                                                        skip_group_check=True)
                        else:
                            last = nc.tensor.matmul(agg(h)[:, 0:1], m.zeros[:, 0:z.NT], m.ones[:, 0:1],
                                                    start=False, stop=True, skip_group_check=True)
                        last.then_inc(scattered[h], 1)

                def turn(i):
                    pe.wait_ge(lo_done, 2 * i + 1)
                    for h in range(2):
                        pe.wait_ge(sums_done[h], i + 2)
                    for k in range(z.KD):
                        for h in range(2):
                            at = (k % (z.KD // 2)) * z.W + h * z.NT
                            last = nc.tensor.transpose(turn_ps[:, k // (z.KD // 2), at:at + z.NT],
                                                       sums[h][:, k * P:(k + 1) * P], m.ident[0:z.NT, 0:z.NT])
                    last.then_inc(turned, 1)

                def product(i):
                    pe.wait_ge(lo_done, 2 * i + 3)
                    for b in range(HALVES):
                        pe.wait_ge(product_out, HALVES * i + b + 1)
                        for o in (2 * b, 2 * b + 1):
                            out = prod_ps[:, b % 2, (o % 2) * z.W:(o % 2 + 1) * z.W]
                            parts = [(w, s, k) for k in range(z.KD)
                                     for w, s in ((w_hi, sumsT_hi), (w_hi, sumsT_lo), (w_lo, sumsT_hi))]
                            for n, (w, s, k) in enumerate(parts):
                                last = nc.tensor.matmul(out, w[:, k, o * P:(o + 1) * P], s[:, k, :], start=n == 0,
                                                        stop=n == len(parts) - 1)
                        last.then_inc(product_done, 1)

                if layer == 0:
                    nc.tensor.matmul(count_ps[0:z.NT, 0:z.TILES], m.zeros[:, 0:z.NT], m.ones[:],
                                     start=True, stop=False, skip_group_check=True)
                scatter(0, 0)
                scatter(0, 1)
                with pe.Fori(1, z.PAIRS) as i:
                    scatter(i, 0)
                    turn(i - 1)
                    scatter(i, 1)
                    product(i - 1)
                turn(z.PAIRS - 1)
                product(z.PAIRS - 1)

            @block.scalar
            def _(act):
                nc.scalar.sem_inc(product_out, 2)
                nc.scalar.sem_inc(stored, 16)
                groups = act.value_load(m.control[0:1, z.TILES:z.TILES + 1], min_val=1, max_val=z.ALL_GROUPS)
                FIRST_BANKS, LAST_BANK = range(HALVES - 1), range(HALVES - 1, HALVES)

                def high_part(i):
                    act.wait_ge(turned, i + 2)
                    act.wait_ge(product_done, HALVES * i + 1)
                    for b in range(2):
                        nc.scalar.activation(
                            sumsT_hi[:, b * z.KD // 2:(b + 1) * z.KD // 2, :],
                            turn_ps[:, b, 0:z.W * z.KD // 2].rearrange("p (k n) -> p k n", n=z.W),
                            ACT.Copy).then_inc(hi_done, 1)

                def split(i, h):
                    with act.Fori(0, groups) as g:
                        split_rows(act.snap(tiles(i, h) * groups + g), range(SPLIT))

                def split_rows(group, chunks):
                    act.wait_ge(split_used, group + 1)
                    for k in chunks:
                        act.wait_ge(gathered[k], 16 * group + 16)
                        nc.scalar.activation(rows_hi[:, k, :], rows[:, k, :], ACT.Copy).then_inc(split_hi, 1)

                def read_product(i, banks):
                    if layer == 0 and 0 in banks:
                        act.wait_ge(stored, 16 * i + 16)
                        act.wait_ge(stats_done, i + 1)
                    for b in banks:
                        act.wait_ge(product_done, HALVES * i + b + 2)
                        for o in (2 * b, 2 * b + 1):
                            from_ = prod_ps[:, b % 2, (o % 2) * z.W:(o % 2 + 1) * z.W]
                            if layer == 0:
                                nc.scalar.activation(hidden[:, o, :], from_, ACT.Identity,
                                                     bias=m.b1[:, o:o + 1]).then_inc(out_done, 1)
                            else:
                                nc.scalar.activation(m.h3T[:, o, bass.ds(i * z.W, z.W)], from_, ACT.Relu,
                                                     bias=m.b3[:, o:o + 1]).then_inc(out_done, 1)
                        act.wait_ge(out_done, KM * i + 2 * b + 2)
                        nc.scalar.sem_inc(product_out, 1)
                    if layer == 0 and HALVES - 1 in banks:
                        act.dma_start(m.hidden_d[bass.ds(i * P, P), :], hidden[:].rearrange("p k n -> p (k n)")).then_inc(stored, 16)

                split(0, 0)
                split(0, 1)
                split(1, 0)
                with act.Fori(1, z.PAIRS - 1) as i:
                    split(i, 1)
                    high_part(i - 1)
                    read_product(i - 1, FIRST_BANKS)
                    split(i + 1, 0)
                    read_product(i - 1, LAST_BANK)
                split(z.PAIRS - 1, 1)
                high_part(z.PAIRS - 2)
                read_product(z.PAIRS - 2, range(HALVES))
                high_part(z.PAIRS - 1)
                read_product(z.PAIRS - 1, range(HALVES))
                if layer == 0:
                    act.wait_ge(stored, 16 * z.PAIRS + 16)


def batch_norm_constants(nc, z, m, dve_sem, act_sem, dve, act, stats, gamma, beta, scale, bias, blocks, tmp):
    if dve is not None:
        for k in range(blocks):
            last = nc.vector.bn_aggr(tmp[:, k, 0:2], stats[:, k, :])
        last.then_inc(dve_sem, 1)
        dve.wait_ge(act_sem, 1)
        nc.vector.reciprocal(scale[:], tmp[:, :, 2]).then_inc(dve_sem, 1)
        dve.wait_ge(dve_sem, 2)
        nc.vector.tensor_tensor(scale[:], scale[:], gamma[:], ALU.mult).then_inc(dve_sem, 1)
        dve.wait_ge(dve_sem, 3)
        nc.vector.tensor_tensor(bias[:], tmp[:, :, 0], scale[:], ALU.mult).then_inc(dve_sem, 1)
        dve.wait_ge(dve_sem, 4)
        nc.vector.tensor_tensor(bias[:], beta[:], bias[:], ALU.subtract).then_inc(dve_sem, 1)
    if act is not None:
        act.wait_ge(dve_sem, 1)
        nc.scalar.activation(tmp[:, :, 2], tmp[:, :, 1], ACT.Sqrt, bias=m.bn_eps[:, 0:1]).then_inc(act_sem, 1)
        act.wait_ge(dve_sem, 5)


def hidden_phase(nc, z, m):
    with ExitStack() as ctx:
        sb = lambda name, shape, dt=F32: ctx.enter_context(nc.sbuf_tensor(name, shape, dt))
        sem = PhaseSemaphores(nc, ctx, "hidden")
        two = lambda name: [sem(f"{name}{q}") for q in range(2)]
        act_f = [sb(f"act_f{q}", [P, z.KH, z.W]) for q in range(2)]
        act_hi = [sb(f"act_hi{q}", [P, z.KH, z.W], F32R) for q in range(2)]
        act_lo = [sb(f"act_lo{q}", [P, z.KH, z.W], F32R) for q in range(2)]
        scale, bias = sb("scale1", [P, z.KH]), sb("bias1", [P, z.KH])
        tmp = sb("bn_tmp1", [P, z.KH, 3])

        loaded = two("loaded")
        rectified = two("rectified")
        hi_done = two("hi_done")
        lo_done = two("lo_done")
        product_done = two("product_done")
        out_done = two("out_done")
        product_out = two("product_out")
        bn_dve, bn_act = sem("bn_dve"), sem("bn_act")

        def out_ps(q, o):
            return m.bank(2 * q + o // 2)[:, (o % 2) * z.W:(o % 2 + 1) * z.W]

        def in_pairs(engine, first, steady, last):
            first()
            with engine.Fori(0, z.PAIRS // 2) as i:
                steady(2 * i, i, i, 0)
                steady(2 * i + 1, i, i + 1, 1)
            last()

        with nc.Block(name="hidden") as block:

            @block.sync
            def _(sp):
                def load(v, u, q):
                    sp.wait_ge(lo_done[q], u + 1)
                    sp.dma_start(act_f[q][:].rearrange("p k n -> p (k n)"),
                                 m.hidden_d[bass.ds(v * P, P), :]).then_inc(loaded[q], 16)

                with sp.Fori(0, z.PAIRS // 2) as i:
                    load(2 * i, i, 0)
                    load(2 * i + 1, i, 1)
                load(z.PAIRS - 1, z.PAIRS // 2, 0)

            @block.scalar
            def _(act):
                for q in range(2):
                    nc.scalar.sem_inc(product_out[q], 1)
                batch_norm_constants(nc, z, m, bn_dve, bn_act, None, act, m.stats1, m.g1, m.be1, scale, bias, z.KH, tmp)

                def prepare(u, q):
                    act.wait_ge(loaded[q], 16 * u + 16)
                    for k in range(z.KH):
                        last = nc.scalar.activation(act_f[q][:, k, :], act_f[q][:, k, :], ACT.Relu,
                                                    scale=scale[:, k:k + 1], bias=bias[:, k:k + 1])
                    last.then_inc(rectified[q], 1)
                    act.wait_ge(rectified[q], u + 1)
                    act.wait_ge(product_done[q], u + 1)
                    nc.scalar.activation(act_hi[q][:], act_f[q][:], ACT.Copy).then_inc(hi_done[q], 1)

                def read_out(v, u, q):
                    act.wait_ge(product_done[q], u + 2)
                    for o in range(z.KD):
                        nc.scalar.activation(m.h2T[:, o, bass.ds(v * z.W, z.W)], out_ps(q, o), ACT.Identity,
                                             bias=m.b2[:, o:o + 1]).then_inc(out_done[q], 1)
                    act.wait_ge(out_done[q], z.KD * u + z.KD)
                    nc.scalar.sem_inc(product_out[q], 1)

                def steady(v, u, next_u, q):
                    prepare(next_u if q == 0 else next_u, 1 - q)
                    read_out(v, u, q)

                in_pairs(act, lambda: prepare(0, 0), steady,
                         lambda: read_out(z.PAIRS - 1, z.PAIRS // 2, 0))

            @block.vector
            def _(dve):
                for q in range(2):
                    nc.vector.sem_inc(lo_done[q], 1)
                batch_norm_constants(nc, z, m, bn_dve, bn_act, dve, None, m.stats1, m.g1, m.be1, scale, bias, z.KH, tmp)

                def low_part(u, q):
                    dve.wait_ge(hi_done[q], u + 1)
                    nc.vector.tensor_tensor(act_lo[q][:], act_f[q][:], act_hi[q][:].bitcast(F32),
                                            ALU.subtract).then_inc(lo_done[q], 1)

                def statistics(v, u, q):
                    for o in range(z.KD):
                        dve.wait_ge(out_done[q], z.KD * u + o + 1)
                        nc.vector.bn_stats(m.stats2[:, o, bass.ds(v * 6, 6)], m.h2T[:, o, bass.ds(v * z.W, z.W)])

                def steady(v, u, next_u, q):
                    low_part(next_u, 1 - q)
                    statistics(v, u, q)

                in_pairs(dve, lambda: low_part(0, 0), steady,
                         lambda: statistics(z.PAIRS - 1, z.PAIRS // 2, 0))

            @block.tensor
            def _(pe):
                for q in range(2):
                    nc.tensor.sem_inc(product_done[q], 1)

                def product(u, q):
                    pe.wait_ge(lo_done[q], u + 2)
                    pe.wait_ge(product_out[q], u + 1)
                    for o in range(z.KD):
                        parts = [(w, s, k) for k in range(z.KH) for w, s in (
                            (m.w2_hi, act_hi[q]), (m.w2_hi, act_lo[q]), (m.w2_lo, act_hi[q]))]
                        for n, (w, s, k) in enumerate(parts):
                            last = nc.tensor.matmul(out_ps(q, o), w[:, k, o * P:(o + 1) * P], s[:, k, :],
                                                    start=n == 0, stop=n == len(parts) - 1)
                    last.then_inc(product_done[q], 1)

                with pe.Fori(0, z.PAIRS // 2) as i:
                    product(i, 0)
                    product(i, 1)
                product(z.PAIRS // 2, 0)


def rows_phase(nc, z, m, layer):
    featT, stats = (m.h2T, m.stats2) if layer == 0 else (m.h3T, m.stats3)
    gamma, beta = (m.g2, m.be2) if layer == 0 else (m.g3, m.be3)
    table, out_d = (m.x_d, m.x1_d) if layer == 0 else (m.x1_d, m.out_d)
    times = 2.0 if layer == 0 else 1.0
    U = z.STEP_TILES
    STEPS = z.TILES // U
    SW = U * z.NT
    PARTS = 16 * len(sprayed(z.NT))
    with ExitStack() as ctx:
        sb = lambda name, shape, dt=F32: ctx.enter_context(nc.sbuf_tensor(f"{name}_r{layer}", shape, dt))
        sem = PhaseSemaphores(nc, ctx, f"rows{layer}")
        each = lambda name: [sem(f"{name}{u}") for u in range(U)]
        normed = sb("normed", [P, z.KD, SW])
        own = [sb(f"own{u}", [z.NT, z.D]) for u in range(U)]
        y = [sb(f"y{u}", [z.NT, z.D]) for u in range(U)]
        done = [sb(f"done{u}", [z.NT, z.D]) for u in range(U)]
        six = sb("six", [z.NT, U, 6])
        mean_var = sb("mean_var", [z.NT, U, 2])
        deviation = sb("deviation", [z.NT, U])
        inverse = sb("inverse", [z.NT, U])
        offset = sb("offset", [z.NT, U])
        scale, bias = sb("scale", [P, z.KD]), sb("bias", [P, z.KD])
        tmp = sb("bn_tmp", [P, z.KD, 3])
        if layer == 0:
            w3_in = sb("w3_in", [P, z.KD, z.D])

        own_in = each("own_in")
        normed_done = sem("normed_done")
        turned = each("turned")
        all_turned = sem("all_turned")
        y_done = each("y_done")
        six_done = each("six_done")
        aggr_done = sem("aggr_done")
        deviation_done, inverse_done, offset_done = sem("deviation_done"), sem("inverse_done"), sem("offset_done")
        norm_done = each("norm_done")
        stored = each("stored")
        waited = sem("waited")
        bn_dve, bn_act = sem("bn_dve"), sem("bn_act")
        if layer == 0:
            w3_loaded, w3_turned = sem("w3_loaded"), sem("w3_turned")
            w3_hi_done, w3_lo_done = sem("w3_hi_done"), sem("w3_lo_done")

        with nc.Block(name=f"rows{layer}") as block:

            @block.sync
            def _(sp):
                for u in range(U):
                    nc.sync.sem_inc(stored[u], PARTS)

                def load(i):
                    for u in range(U):
                        sp.wait_ge(y_done[u], i + 1)
                        for a, b in sprayed(z.NT):
                            sp.dma_start(own[u][a:b, :], table[bass.ds((i * U + u) * z.NT + a, b - a), :]
                                         ).then_inc(own_in[u], 16)

                def store(i):
                    for u in range(U):
                        sp.wait_ge(norm_done[u], i + 2)
                        for a, b in sprayed(z.NT):
                            sp.dma_start(out_d[bass.ds((i * U + u) * z.NT + a, b - a), :], done[u][a:b, :]
                                         ).then_inc(stored[u], 16)

                load(0)
                if layer == 0:
                    sp.dma_start(w3_in[:], m.w3_d.rearrange("(k p) n -> p k n", p=P)).then_inc(w3_loaded, 16)
                load(1)
                with sp.Fori(2, STEPS) as i:
                    load(i)
                    store(i - 2)
                store(STEPS - 2)
                store(STEPS - 1)
                for u in range(U):
                    sp.wait_ge(stored[u], PARTS * (STEPS + 1))

            @block.scalar
            def _(act):
                for u in range(U):
                    nc.scalar.sem_inc(norm_done[u], 1)
                batch_norm_constants(nc, z, m, bn_dve, bn_act, None, act, stats, gamma, beta, scale, bias, z.KD, tmp)

                def features(i):
                    act.wait_ge(all_turned, i + 1)
                    for k in range(z.KD):
                        last = nc.scalar.activation(normed[:, k, :], featT[:, k, bass.ds(i * SW, SW)],
                                                    ACT.Relu if layer == 0 else ACT.Identity,
                                                    scale=scale[:, k:k + 1], bias=bias[:, k:k + 1])
                    last.then_inc(normed_done, 1)

                def rows(i):
                    act.wait_ge(aggr_done, i + 1)
                    nc.scalar.activation(deviation[:], mean_var[:, :, 1], ACT.Sqrt,
                                         bias=m.ln_eps[0:z.NT, 0:1]).then_inc(deviation_done, 1)
                    act.wait_ge(offset_done, i + 1)
                    for u in range(U):
                        act.wait_ge(stored[u], PARTS * (i + 1))
                        nc.scalar.activation(done[u][:], y[u][:], ACT.Identity, scale=inverse[:, u:u + 1],
                                             bias=offset[:, u:u + 1]).then_inc(norm_done[u], 1)

                features(0)
                if layer == 0:
                    for k in range(z.KD):
                        act.wait_ge(w3_turned, k + 1)
                        nc.scalar.activation(m.w3_hi[:, k, :], m.bank(W3_BANK), ACT.Copy).then_inc(w3_hi_done, 1)
                with act.Fori(1, STEPS) as i:
                    features(i)
                    rows(i - 1)
                rows(STEPS - 1)

            @block.tensor
            def _(pe):
                nc.tensor.sem_inc(all_turned, 1)

                def turn(i):
                    pe.wait_ge(normed_done, i + 1)
                    for u in range(U):
                        pe.wait_ge(y_done[u], i + 1)
                        for k in range(z.KD):
                            last = nc.tensor.transpose(m.bank(u)[0:z.NT, k * P:(k + 1) * P],
                                                       normed[:, k, u * z.NT:(u + 1) * z.NT], m.ident[:])
                        last.then_inc(turned[u], 1)
                    pe.wait_ge(turned[U - 1], i + 1)
                    nc.tensor.sem_inc(all_turned, 1)

                turn(0)
                if layer == 0:
                    pe.wait_ge(w3_loaded, 16)
                    for k in range(z.KD):
                        if k:
                            pe.wait_ge(w3_lo_done, k)
                        for o in range(z.KD):
                            last = nc.tensor.transpose(m.bank(W3_BANK)[:, o * P:(o + 1) * P],
                                                       w3_in[:, o, k * P:(k + 1) * P], m.ident[:])
                        last.then_inc(w3_turned, 1)
                with pe.Fori(1, STEPS) as i:
                    turn(i)

            @block.vector
            def _(dve):
                for u in range(U):
                    nc.vector.sem_inc(y_done[u], 1)
                batch_norm_constants(nc, z, m, bn_dve, bn_act, dve, None, stats, gamma, beta, scale, bias, z.KD, tmp)

                def inverses(i):
                    dve.wait_ge(deviation_done, i + 1)
                    nc.vector.reciprocal(inverse[:], deviation[:]).then_inc(inverse_done, 1)
                    dve.wait_ge(inverse_done, i + 1)
                    nc.vector.scalar_tensor_tensor(offset[:], mean_var[:, :, 0], -1.0, inverse[:], ALU.mult,
                                                   ALU.mult).then_inc(offset_done, 1)

                def sums(i, u):
                    dve.wait_ge(own_in[u], PARTS * (i + 1))
                    dve.wait_ge(turned[u], i + 1)
                    dve.wait_ge(norm_done[u], i + 1)
                    nc.vector.scalar_tensor_tensor(y[u][:], own[u][:], times, m.bank(u)[0:z.NT, 0:z.D],
                                                   ALU.mult, ALU.add).then_inc(y_done[u], 1)

                def moments(i, u):
                    dve.wait_ge(y_done[u], i + 2)
                    nc.vector.bn_stats(six[:, u, :], y[u][:]).then_inc(six_done[u], 1)

                def mean_variance(i, u):
                    dve.wait_ge(six_done[u], i + 1)
                    nc.vector.sem_inc(waited, 1)
                    last = nc.vector.bn_aggr(mean_var[:, u, :], six[:, u, :])
                    if u == U - 1:
                        last.then_inc(aggr_done, 1)

                def step(i):
                    for n in range(U + 2):
                        if n < U:
                            sums(i, n)
                        if 0 <= n - 2:
                            mean_variance(i, n - 2)
                        if 0 <= n - 1 < U:
                            moments(i, n - 1)

                step(0)
                if layer == 0:
                    for k in range(z.KD):
                        dve.wait_ge(w3_hi_done, k + 1)
                        nc.vector.tensor_tensor(m.w3_lo[:, k, :], m.bank(W3_BANK), m.w3_hi[:, k, :].bitcast(F32),
                                                ALU.subtract).then_inc(w3_lo_done, 1)
                with dve.Fori(1, STEPS) as i:
                    inverses(i - 1)
                    step(i)
                inverses(STEPS - 1)


class Memory:
    pass


def gnn_kernel(nc, x, src, dst, eps, w1, b1, g1, be1, w2, b2, g2, be2, w3, b3, g3, be3, out):
    z = Shapes(x.shape[0], x.shape[1], src.shape[0], w1.shape[1])
    m = Memory()
    m.x_d, m.src_d, m.dst_d, m.eps_d, m.w1_d, m.w2_d, m.w3_d, m.out_d = x, src, dst, eps, w1, w2, w3, out
    m.b1_d, m.g1_d, m.be1_d, m.b2_d, m.g2_d, m.be2_d, m.b3_d, m.g3_d, m.be3_d = b1, g1, be1, b2, g2, be2, b3, g3, be3
    m.src_pad = nc.dram_tensor("src_pad", (z.E + z.GROUP,), I32, kind="Internal").ap()
    m.dst_pad = nc.dram_tensor("dst_pad", (z.E + z.GROUP,), I32, kind="Internal").ap()
    m.hidden_d = nc.dram_tensor("hidden_d", (z.PAIRS * P, z.KH * z.W), F32, kind="Internal").ap()
    m.x1_d = nc.dram_tensor("x1_d", (z.N, z.D), F32, kind="Internal").ap()
    with ExitStack() as ctx:
        def sb(name, shape, dt=F32, side="left", scope=ctx):
            return scope.enter_context(nc.sbuf_tensor(name, shape, dt, side=side))

        psum = ctx.enter_context(nc.psum_tensor("psum", [P, 8, 512], F32))
        m.bank = lambda b: psum[:, b, :]
        m.banks = lambda a, b: psum[:, a:b, :]
        m.column_ps = psum[:, 6, 0:z.NT]
        m.column, m.ident = sb("column", [P, P]), sb("ident", [P, P])
        m.self_weight, m.zeros, m.ones = sb("self_weight", [P, 1]), sb("zeros", [P, P], BF16), sb("ones", [P, z.TILES], BF16)
        m.tile_base, m.lone = sb("tile_base", [P, z.TILES]), sb("lone", [z.NT, z.TILES])
        m.control = sb("control", [1, z.TILES + 1], I32)
        m.bn_eps, m.ln_eps = sb("bn_eps", [P, 1]), sb("ln_eps", [P, 1])
        m.b1, m.g1, m.be1 = (sb(n, [P, z.KH]) for n in ("b1", "g1", "be1"))
        m.b2, m.g2, m.be2, m.b3, m.g3, m.be3 = (sb(n, [P, z.KD]) for n in ("b2", "g2", "be2", "b3", "g3", "be3"))
        m.stats1 = sb("stats1", [P, z.KH, z.PAIRS * 6])
        m.stats2 = sb("stats2", [P, z.KD, z.PAIRS * 6])
        m.stats3 = sb("stats3", [P, z.KD, z.PAIRS * 6])

        with ExitStack() as second:
            m.w2_hi = sb("w2_hi", [P, z.KH, z.D], F32R, scope=second)
            m.w2_lo = sb("w2_lo", [P, z.KH, z.D], F32R, scope=second)
            with ExitStack() as first:
                m.w1_hi = sb("w1_hi", [P, z.KD, z.H], F32R, scope=first)
                m.w1_lo = sb("w1_lo", [P, z.KD, z.H], F32R, scope=first)
                setup_phase(nc, z, m)
                gather_phase(nc, z, m, 0)
            features = ExitStack()
            m.h2T = sb("h2T", [P, z.KD, z.N], side="right", scope=features)
            hidden_phase(nc, z, m)
        m.w3_hi, m.w3_lo = sb("w3_hi", [P, z.KD, z.D], F32R), sb("w3_lo", [P, z.KD, z.D], F32R)
        rows_phase(nc, z, m, 0)
        features.close()
        m.h3T = sb("h3T", [P, z.KD, z.N], side="right")
        gather_phase(nc, z, m, 1)
        rows_phase(nc, z, m, 1)


_INS = ["x", "src", "dst", "L0_gnn_eps", "L0_gnn_W1", "L0_gnn_b1", "L0_gnn_g1", "L0_gnn_be1", "L0_gnn_W2",
        "L0_gnn_b2", "L0_gnn_g2", "L0_gnn_be2", "L1_gnn_W", "L1_gnn_b", "L1_gnn_gamma", "L1_gnn_beta"]


def kernel(**inputs):
    import numpy as np
    import concourse.bacc as bacc
    from concourse.bass_utils import run_bass_kernel_spmd

    nc = bacc.Bacc("TRN2", target_bir_lowering=False, num_devices=1)
    arrays, args = {}, []
    for name in _INS:
        a = np.asarray(inputs[name])
        a = np.ascontiguousarray(a.reshape((1,)) if a.ndim == 0 else a)
        arrays[f"{name}_in"] = a
        args.append(nc.dram_tensor(f"{name}_in", a.shape, mybir.dt.from_np(a.dtype), kind="ExternalInput").ap())
    args.append(nc.dram_tensor("rows_out", arrays["x_in"].shape, F32, kind="ExternalOutput").ap())
    gnn_kernel(nc, *args)
    return run_bass_kernel_spmd(nc, [arrays], core_ids=[0]).results[0]["rows_out"]
```

```python
import concourse.bass as bass
from concourse import mybir
from contextlib import ExitStack

F32 = mybir.dt.float32
F32R = mybir.dt.float32r
BF16 = mybir.dt.bfloat16
I32 = mybir.dt.int32
ALU = mybir.AluOpType
ACT = mybir.ActivationFunctionType
AX = mybir.AxisListType
BN_EPS = 1e-05
LN_EPS = 1e-05
P = 128


class Shapes:

    def __init__(self, n, d, e, h):
        self.N, self.D, self.E, self.H = n, d, e, h
        self.NT = max(k for k in range(1, P + 1) if n % (2 * k) == 0 and (n // (2 * k)) % 2 == 1)
        self.TILES = n // self.NT
        self.PAIRS = self.TILES // 2
        self.W = 2 * self.NT
        self.STEP_TILES = max(k for k in range(1, 6) if self.TILES % k == 0)
        mean = e / self.TILES
        self.CHUNKS = -int(-(mean + 3.5 * mean**0.5) // P)
        self.GROUP = self.CHUNKS * P
        self.MAIN = self.GROUP - P
        self.ALL_GROUPS = -(-e // self.GROUP)
        self.SPLIT = (self.CHUNKS * 7 // 17, max(1, self.CHUNKS * 2 // 17))
        self.SLOT_BLOCKS = 4
        self.EP = max(k for k in range(1, P + 1) if e % k == 0)
        self.EC = e // self.EP
        self.KD = d // P
        self.KH = h // P

    def blocks(self, layer):
        first, whole = self.SPLIT[layer], self.CHUNKS - 1 - self.SPLIT[layer]
        return [first + -(-whole * b // self.SLOT_BLOCKS) for b in range(self.SLOT_BLOCKS)]

    def order(self, layer):
        split, whole = list(range(self.SPLIT[layer])), list(range(self.SPLIT[layer], self.CHUNKS - 1))
        order = whole[:2]
        for n, k in enumerate(whole[2:]):
            order += split[n:n + 1] + [k]
        return order + split[len(whole) - 2:]


def sprayed(count):
    most = count // 16 * 16
    return [part for part in ((0, most), (most, count)) if part[0] < part[1]]


class PhaseSemaphores:

    def __init__(self, nc, ctx, label):
        self.nc, self.label, self.sems = nc, label, []
        ctx.callback(self.clear)

    def __call__(self, name):
        self.sems.append(self.nc.alloc_semaphore(f"{self.label}_{name}"))
        return self.sems[-1]

    def clear(self):
        self.nc.clear_and_free_semaphores(self.sems)
        self.nc.all_engine_barrier()


def setup_phase(nc, z, m):
    with ExitStack() as ctx:
        sb = lambda name, shape, dt=F32: ctx.enter_context(nc.sbuf_tensor(name, shape, dt))
        sem = PhaseSemaphores(nc, ctx, "setup")
        T = z.TILES
        dst_i = sb("dst_i", [z.EP, z.EC], I32)
        next_i = sb("next_i", [z.EP, z.EC], I32)
        falls = sb("falls", [z.EP, z.EC])
        fall_count = sb("fall_count", [z.EP, 1])
        first_f = sb("first_f", [z.EP, 1])
        is_before = sb("is_before", [z.EP, T])
        part_f = sb("part_f", [T, 1])
        part_i = sb("part_i", [T, 1], I32)
        part_edges = sb("part_edges", [T, z.EC], I32)
        edge_before = sb("edge_before", [T, z.EC])
        inside = sb("inside", [T, 1])
        start_col = sb("start_col", [T, 1])
        first_node = sb("first_node", [P, 1])
        starts = sb("starts", [1, T + 1])
        sizes = sb("sizes", [1, T])
        over = sb("over", [1, T])
        last_chunk = sb("last_chunk", [1, T])
        prefix = sb("prefix", [1, 2, T])
        flags = sb("flags", [1, 4])
        fill = sb("fill", [1, 2, z.GROUP], I32)
        eps_in = sb("eps_in", [P, 1])
        ones_col = sb("ones_col", [P, 1])
        partition = sb("partition", [P, 1])
        parts_ps, falls_ps, starts_ps = m.bank(0)[0:T, 0:1], m.bank(1)[0:1, 0:1], m.bank(2)[0:1, 0:T]

        copied = sem("edges_copied")
        edges_in = sem("edges_in")
        next_in = sem("next_in")
        small_in = sem("small_in")
        filled = sem("filled")
        tables = sem("tables")
        compared = sem("compared")
        parts_counted = sem("parts_counted")
        part_known = sem("part_known")
        part_in = sem("part_in")
        start_known = sem("start_known")
        falls_done, falls_counted = sem("falls_done"), sem("falls_counted")
        starts_turned = sem("starts_turned")
        waited = sem("waited")
        dve_step = sem("dve_step")
        EDGE_PARTS = 16 * len(sprayed(z.EP))
        NEXT_PARTS = 16 * (len(sprayed(z.EP - 1)) + 2)
        small = [(m.b1, m.b1_d), (m.g1, m.g1_d), (m.be1, m.be1_d), (m.b2, m.b2_d), (m.g2, m.g2_d),
                 (m.be2, m.be2_d), (m.b3, m.b3_d), (m.g3, m.g3_d), (m.be3, m.be3_d)]

        with nc.Block(name="setup") as block:

            @block.sync
            def _(sp):
                edges = m.dst_d.rearrange("(p c) -> p c", p=z.EP)
                for a, b in sprayed(z.EP):
                    sp.dma_start(dst_i[a:b, :], edges[a:b, :]).then_inc(edges_in, 16)
                full = (z.EP - 1) * z.EC
                after = m.dst_d[1:full + 1].rearrange("(p c) -> p c", p=z.EP - 1)
                for a, b in sprayed(z.EP - 1):
                    sp.dma_start(next_i[a:b, :], after[a:b, :]).then_inc(next_in, 16)
                sp.dma_start(next_i[z.EP - 1:z.EP, 0:z.EC - 1], m.dst_d[full + 1:z.E][None, :]).then_inc(next_in, 16)
                sp.wait_ge(filled, 1)
                sp.dma_start(next_i[z.EP - 1:z.EP, z.EC - 1:z.EC], fill[:, 1, 0:1]).then_inc(next_in, 16)
                for pad, edges, f in ((m.src_pad, m.src_d, 0), (m.dst_pad, m.dst_d, 1)):
                    sp.dma_start(pad[0:z.E].rearrange("(p c) -> p c", p=16), edges.rearrange("(p c) -> p c", p=16)
                                 ).then_inc(copied, 16)
                    sp.dma_start(pad[z.E:z.E + z.GROUP][None, :], fill[:, f, :]).then_inc(copied, 16)
                sp.wait_ge(copied, 64)

            @block.scalar
            def _(act):
                with nc.allow_non_contiguous_dma(reason="vectors to one value a partition"):
                    act.dma_start(eps_in[:], m.eps_d.partition_broadcast(P)).then_inc(small_in, 16)
                    for vec, dram in small:
                        act.dma_start(vec[:], dram.rearrange("(m p) -> p m", p=P)).then_inc(small_in, 16)
                act.wait_ge(small_in, 16 * (1 + len(small)))

            @block.gpsimd
            def _(pool):
                nc.gpsimd.memset(fill[:, 0, :], 0)
                nc.gpsimd.memset(fill[:, 1, :], z.N).then_inc(filled, 1)
                nc.gpsimd.iota(m.tile_base[:], [[z.NT, T]], base=0, channel_multiplier=0,
                               allow_small_or_imprecise_dtypes=True)
                nc.gpsimd.memset(ones_col[:], 1.0)
                nc.gpsimd.iota(first_node[:], [[0, 1]], base=0, channel_multiplier=z.NT,
                               allow_small_or_imprecise_dtypes=True)
                nc.gpsimd.iota(m.column[:], [[1, P]], base=0, channel_multiplier=0,
                               allow_small_or_imprecise_dtypes=True)
                nc.gpsimd.iota(partition[:], [[0, 1]], base=0, channel_multiplier=1,
                               allow_small_or_imprecise_dtypes=True).then_inc(tables, 1)
                nc.gpsimd.memset(m.zeros[:], 0.0)
                nc.gpsimd.memset(m.ones[:], 1.0)
                nc.gpsimd.memset(m.bn_eps[:], BN_EPS)
                nc.gpsimd.memset(m.ln_eps[:], LN_EPS)
                pool.wait_ge(part_known, 1)
                nc.gpsimd.sem_inc(waited, 1)
                nc.gpsimd.indirect_dma_start(
                    part_edges[:], None, m.dst_d.rearrange("(p c) -> p c", p=z.EP),
                    bass.IndirectOffsetOnAxis(ap=part_i[:, 0:1], axis=0)).then_inc(part_in, 16)

            @block.tensor
            def _(pe):
                pe.wait_ge(compared, 1)
                nc.tensor.matmul(parts_ps, is_before[:], ones_col[0:z.EP, :], start=True, stop=True
                                 ).then_inc(parts_counted, 1)
                pe.wait_ge(falls_done, 1)
                nc.tensor.matmul(falls_ps, fall_count[:], ones_col[0:z.EP, :], start=True, stop=True
                                 ).then_inc(falls_counted, 1)
                pe.wait_ge(start_known, 1)
                nc.tensor.transpose(starts_ps, start_col[:], m.ident[0:T, 0:T]).then_inc(starts_turned, 1)

            @block.vector
            def _(dve):
                step = [0]

                def link(instruction):
                    step[0] += 1
                    instruction.then_inc(dve_step, 1)
                    dve.wait_ge(dve_step, step[0])

                dve.wait_ge(tables, 1)
                nc.vector.tensor_scalar(m.ident[:], m.column[:], partition[:, 0:1], None, ALU.is_equal)
                nc.vector.tensor_copy(m.column_ps, m.column[:, 0:z.NT])
                nc.vector.memset(starts[:, T:T + 1], float(z.E))
                dve.wait_ge(edges_in, EDGE_PARTS)
                link(nc.vector.tensor_copy(first_f[:], dst_i[:, 0:1]))
                nc.vector.tensor_scalar(is_before[:], m.tile_base[0:z.EP, :], first_f[:, 0:1], None,
                                        ALU.is_gt).then_inc(compared, 1)
                dve.wait_ge(parts_counted, 1)
                link(nc.vector.tensor_scalar(part_f[:], parts_ps, -1.0, 0.0, ALU.add, ALU.max))
                nc.vector.tensor_copy(part_i[:], part_f[:]).then_inc(part_known, 1)
                dve.wait_ge(next_in, NEXT_PARTS)
                link(nc.vector.tensor_tensor(falls[:], dst_i[:], next_i[:], ALU.is_gt))
                nc.vector.tensor_reduce(fall_count[:], falls[:], AX.X, ALU.add).then_inc(falls_done, 1)
                dve.wait_ge(small_in, 16 * (1 + len(small)))
                nc.vector.tensor_scalar(m.self_weight[:], eps_in[:], 1.0, None, ALU.add)
                dve.wait_ge(part_in, 16)
                link(nc.vector.tensor_scalar(edge_before[:], part_edges[:], first_node[0:T, 0:1], None, ALU.is_lt,
                                             ALU.add, accum_out=inside[:]))
                nc.vector.scalar_tensor_tensor(start_col[:], part_f[:], float(z.EC), inside[:], ALU.mult,
                                               ALU.add).then_inc(start_known, 1)
                dve.wait_ge(starts_turned, 1)
                link(nc.vector.tensor_copy(starts[:, 0:T], starts_ps))
                link(nc.vector.tensor_tensor(sizes[:], starts[:, 1:T + 1], starts[:, 0:T], ALU.subtract))
                nc.vector.tensor_scalar(last_chunk[:], sizes[:], float(z.MAIN), None, ALU.is_gt)
                link(nc.vector.tensor_scalar(over[:], sizes[:], float(z.GROUP), None, ALU.is_gt))
                link(nc.vector.tensor_reduce(flags[:, 0:1], over[:], AX.X, ALU.max))
                dve.wait_ge(falls_counted, 1)
                link(nc.vector.tensor_tensor(flags[:, 1:2], flags[:, 0:1], falls_ps, ALU.add))
                link(nc.vector.tensor_scalar(flags[:, 1:2], flags[:, 1:2], 1.0, None, ALU.min))
                nc.vector.tensor_scalar(flags[:, 2:3], flags[:, 1:2], -1.0, 1.0, ALU.mult, ALU.add)
                nc.vector.tensor_scalar(last_chunk[:], last_chunk[:], flags[:, 1:2], None, ALU.max)
                link(nc.vector.tensor_scalar(flags[:, 3:4], flags[:, 1:2], float(z.ALL_GROUPS - 1), 1.0,
                                             ALU.mult, ALU.add))
                nc.vector.tensor_scalar(m.starts, starts[:, 0:T], flags[:, 2:3], None, ALU.mult)
                nc.vector.tensor_copy(m.groups, flags[:, 3:4])
                nc.vector.tensor_copy(m.last_chunk, last_chunk[:])
                link(nc.vector.tensor_copy(prefix[:, 0, :], last_chunk[:]))
                reach, now = 1, 0
                while reach < T:
                    nc.vector.tensor_copy(prefix[:, 1 - now, 0:reach], prefix[:, now, 0:reach])
                    link(nc.vector.tensor_tensor(prefix[:, 1 - now, reach:], prefix[:, now, reach:],
                                                 prefix[:, now, 0:T - reach], ALU.add))
                    reach, now = 2 * reach, 1 - now
                link(nc.vector.tensor_tensor(sizes[:], prefix[:, now, :], last_chunk[:], ALU.subtract))
                nc.vector.tensor_scalar(m.last_before, sizes[:], flags[:, 3:4], None, ALU.mult)


def gather_phase(nc, z, m, layer):
    KM = z.KH if layer == 0 else z.KD
    OWN_PARTS = 16 * len(sprayed(z.NT))
    SPLIT = z.SPLIT[layer]
    BLOCKS = z.blocks(layer)
    LAST = z.CHUNKS - 1
    HALVES = KM // 2
    w_hi, w_lo = (m.w1_hi, m.w1_lo) if layer == 0 else (m.w3_hi, m.w3_lo)
    table = m.x_d if layer == 0 else m.x1_d
    stats = m.stats1 if layer == 0 else m.stats3
    with ExitStack() as ctx:
        sb = lambda name, shape, dt=F32: ctx.enter_context(nc.sbuf_tensor(f"{name}_{layer}", shape, dt))
        sem = PhaseSemaphores(nc, ctx, f"gather{layer}")
        two = lambda name: [sem(f"{name}{h}") for h in range(2)]
        rows = sb("rows", [P, z.CHUNKS, z.D])
        rows_hi, rows_lo = sb("rows_hi", [P, SPLIT, z.D], F32R), sb("rows_lo", [P, SPLIT, z.D], F32R)
        select = [sb(f"select{h}", [P, z.CHUNKS - SPLIT, z.NT]) for h in range(2)]
        select_r = [sb(f"select_r{h}", [P, SPLIT, z.NT], F32R) for h in range(2)]
        src_i = [sb(f"src_i{h}", [P, z.CHUNKS], I32) for h in range(2)]
        dst_i = [sb(f"dst_i{h}", [P, z.CHUNKS], I32) for h in range(2)]
        local = [sb(f"local{h}", [P, z.CHUNKS]) for h in range(2)]
        own = [sb(f"own{h}", [z.NT, z.D]) for h in range(2)]
        sums = [sb(f"sums{h}", [z.NT, z.D]) for h in range(2)]
        sumsT_hi = sb("sumsT_hi", [P, z.KD, z.W], F32R)
        sumsT_lo = sb("sumsT_lo", [P, z.KD, z.W], F32R)
        if layer == 0:
            hidden = sb("hidden", [P, KM, z.W])
            weight_in = sb("weight_in", [P, max(z.KD * z.H, z.KH * z.D)])
            edge_count = [sb(f"edge_count{h}", [P, 2, z.NT], BF16) for h in range(2)]

        src_in, dst_in = two("src_in"), two("dst_in")
        local_done = two("local_done")
        select_done = two("select_done")
        gathered = [sem(f"gathered{k}") for k in range(z.CHUNKS)]
        split_hi = sem("split_hi")
        split_lo = sem("split_lo")
        split_used = sem("split_used")
        slots_free = sem("slots_free")
        scattered = two("scattered")
        own_in = two("own_in")
        sums_done = two("sums_done")
        turned = sem("turned")
        hi_done = sem("hi_done")
        lo_done = sem("lo_done")
        product_done = sem("product_done")
        product_out = sem("product_out")
        out_done = sem("out_done")
        stats_done = sem("stats_done")
        counted = two("counted")
        waited = sem("waited")
        lone_done = sem("lone_done")
        weights_in = [sem(f"weight{n}_in") for n in range(2 - layer)]
        weights_hi = sem("weights_hi")
        weights_lo = sem("weights_lo")
        weight_turned = sem("weight_turned")
        weight_d = (m.w1_d, m.w2_d) if layer == 0 else (m.w3_d,)
        weight_hi, weight_lo = ((m.w1_hi, m.w2_hi), (m.w1_lo, m.w2_lo)) if layer == 0 else ((m.w3_hi,), (m.w3_lo,))

        def agg(h):
            return m.bank(h)[0:z.NT, :]

        w3_ps = m.banks(2, 2 + z.KD)
        if layer == 1:
            weight_in = m.h3T[:, 0, 0:z.KD * z.D]
        turn_ps = m.banks(2, 4)
        prod_ps = m.banks(4, 6)
        count_ps = m.bank(7)

        def tiles(i, h):
            return 2 * i + h

        def flat(blocks):
            return blocks[:].rearrange("p k n -> p (k n)")

        with nc.Block(name=f"gather{layer}") as block:

            @block.sync
            def _(sp):
                groups = sp.value_load(m.groups, min_val=1, max_val=z.ALL_GROUPS)
                with sp.Fori(0, z.PAIRS) as i:
                    for h in range(2):
                        tile = tiles(i, h)
                        start = sp.value_load(m.starts[:, bass.ds(tile, 1)], min_val=0, max_val=z.E)
                        with sp.Fori(0, groups) as g:
                            use = i * groups + g
                            sp.wait_ge(scattered[h], use + 1)
                            at = nc.s_assert_within(
                                sp.snap(start + g * z.GROUP), 0, z.E, skip_runtime_bounds_check_because=
                                "start is 0 unless there is but one group, and the groups begin before the last edge")
                            for out, edges, landed in ((src_i[h], m.src_pad, src_in[h]), (dst_i[h], m.dst_pad, dst_in[h])):
                                sp.dma_start(out[:, 0:LAST], edges[bass.ds(at, z.MAIN)].rearrange("(p c) -> p c", p=P)
                                             ).then_inc(landed, 16)
                                sp.dma_start(out[:, LAST:], edges[bass.ds(at + z.MAIN, P)].rearrange("(p c) -> p c", p=P)
                                             ).then_inc(landed, 16)
                        sp.wait_ge(sums_done[h], i + 1)
                        for a, b in sprayed(z.NT):
                            sp.dma_start(own[h][a:b, :], table[bass.ds(tile * z.NT + a, b - a), :]).then_inc(own_in[h], 16)

            @block.gpsimd
            def _(pool):
                groups = pool.value_load(m.groups, min_val=1, max_val=z.ALL_GROUPS)

                def gather(h, k):
                    nc.gpsimd.indirect_dma_start(
                        rows[:, k, :], None, table, bass.IndirectOffsetOnAxis(ap=src_i[h][:, k:k + 1], axis=0)
                    ).then_inc(gathered[k], 16)

                with pool.Fori(0, z.PAIRS) as i:
                    for h in range(2):
                        has_last = pool.value_load(m.last_chunk[:, bass.ds(tiles(i, h), 1)], min_val=0, max_val=1)
                        with pool.Fori(0, groups) as g:
                            pool.wait_ge(src_in[h], 32 * (i * groups + g) + 32)
                            group = pool.snap(tiles(i, h) * groups + g)
                            for k in range(LAST):
                                if k == 0 and SPLIT:
                                    pool.wait_ge(split_lo, SPLIT * group + SPLIT)
                                    nc.gpsimd.sem_inc(waited, 1)
                                elif k in BLOCKS:
                                    pool.wait_ge(slots_free, z.SLOT_BLOCKS * group + BLOCKS.index(k) + 1)
                                    nc.gpsimd.sem_inc(waited, 1)
                                gather(h, k)
                            with pool.If(has_last == 1):
                                gather(h, LAST)

            @block.vector
            def _(dve):
                nc.vector.sem_inc(lo_done, 1)
                nc.vector.sem_inc(split_lo, SPLIT)
                nc.vector.sem_inc(stats_done, 1)
                for h in range(2):
                    nc.vector.sem_inc(sums_done[h], 1)
                groups = dve.value_load(m.groups, min_val=1, max_val=z.ALL_GROUPS)
                if layer == 1:
                    nc.vector.tensor_scalar(m.lone[:], count_ps[0:z.NT, 0:z.TILES], 0.0, None,
                                            ALU.is_equal).then_inc(lone_done, 1)
                    dve.wait_ge(lone_done, 1)

                def weight(n):
                    dve.wait_ge(weights_hi, n + 1)
                    nc.vector.tensor_tensor(flat(weight_lo[n]), weight_in[:] if layer == 0 else flat(w3_ps),
                                            flat(weight_hi[n]).bitcast(F32), ALU.subtract).then_inc(weights_lo, 1)

                def selection(i, h):
                    tile = tiles(i, h)
                    with dve.Fori(0, groups) as g:
                        use = dve.snap(i * groups + g)
                        dve.wait_ge(dst_in[h], 32 * use + 32)
                        nc.vector.tensor_scalar(local[h][:], dst_i[h][:], m.tile_base[:, bass.ds(tile, 1)], None,
                                                ALU.subtract).then_inc(local_done[h], 1)
                        dve.wait_ge(local_done[h], use + 1)
                        dve.wait_ge(scattered[h], use + 1)
                        for out, a, b in ((select_r[h], 0, SPLIT), (select[h], SPLIT, z.CHUNKS)):
                            nc.vector.tensor_tensor(
                                out[:], m.column_ps[:, None, :].broadcast_to([P, b - a, z.NT]),
                                local[h][:, a:b, None].broadcast_to([P, b - a, z.NT]), ALU.is_equal
                            ).then_inc(select_done[h], 1)
                        group = dve.snap(tile * groups + g)
                        for k in range(SPLIT):
                            dve.wait_ge(split_hi, group * SPLIT + k + 1)
                            nc.vector.tensor_tensor(rows_lo[:, k, :], rows[:, k, :], rows_hi[:, k, :].bitcast(F32),
                                                    ALU.subtract).then_inc(split_lo, 1)
                        if layer == 0:
                            dve.wait_ge(select_done[h], 2 * use + 2)
                            with nc.allow_low_precision(reason="counts up to CHUNKS are exact in bfloat16"):
                                nc.vector.tensor_reduce(edge_count[h][:, 0, :],
                                                        select_r[h][:].bitcast(F32).rearrange("p k n -> p n k"),
                                                        AX.X, ALU.add)
                                nc.vector.tensor_reduce(edge_count[h][:, 1, :], select[h][:].rearrange("p k n -> p n k"),
                                                        AX.X, ALU.add).then_inc(counted[h], 1)

                def read_sums(i, h):
                    dve.wait_ge(own_in[h], OWN_PARTS * (i + 1))
                    dve.wait_ge(scattered[h], (i + 1) * groups + 1)
                    dve.wait_ge(turned, i + 1)
                    weight = m.self_weight[0:z.NT, :] if layer == 0 else m.lone[:, bass.ds(tiles(i, h), 1)]
                    nc.vector.scalar_tensor_tensor(sums[h][:], own[h][:], weight, agg(h), ALU.mult,
                                                   ALU.add).then_inc(sums_done[h], 1)

                def low_part(i):
                    dve.wait_ge(product_done, HALVES * i + 1)
                    for b in range(2):
                        dve.wait_ge(hi_done, 2 * i + b + 1)
                        half = slice(b * z.KD // 2, (b + 1) * z.KD // 2)
                        nc.vector.tensor_tensor(
                            sumsT_lo[:, half, :], turn_ps[:, b, 0:z.W * z.KD // 2].rearrange("p (k n) -> p k n", n=z.W),
                            sumsT_hi[:, half, :].bitcast(F32), ALU.subtract).then_inc(lo_done, 1)

                def statistics(i):
                    for k in range(KM):
                        dve.wait_ge(out_done, KM * i + k + 1)
                        from_ = hidden[:, k, :] if layer == 0 else m.h3T[:, k, bass.ds(i * z.W, z.W)]
                        last = nc.vector.bn_stats(stats[:, k, bass.ds(i * 6, 6)], from_)
                    last.then_inc(stats_done, 1)

                if layer == 1:
                    weight(0)
                selection(0, 0)
                if layer == 0:
                    weight(0)
                selection(0, 1)
                read_sums(0, 0)
                read_sums(0, 1)
                selection(1, 0)
                with dve.Fori(1, z.PAIRS - 1) as i:
                    selection(i, 1)
                    read_sums(i, 0)
                    low_part(i - 1)
                    read_sums(i, 1)
                    selection(i + 1, 0)
                    statistics(i - 1)
                selection(z.PAIRS - 1, 1)
                read_sums(z.PAIRS - 1, 0)
                low_part(z.PAIRS - 2)
                if layer == 0:
                    weight(1)
                read_sums(z.PAIRS - 1, 1)
                statistics(z.PAIRS - 2)
                low_part(z.PAIRS - 1)
                statistics(z.PAIRS - 1)

            @block.tensor
            def _(pe):
                for h in range(2):
                    nc.tensor.sem_inc(scattered[h], 1)
                nc.tensor.sem_inc(slots_free, z.SLOT_BLOCKS)
                nc.tensor.sem_inc(split_used, SPLIT)
                nc.tensor.sem_inc(turned, 1)
                nc.tensor.sem_inc(product_done, 1)
                groups = pe.value_load(m.groups, min_val=1, max_val=z.ALL_GROUPS)

                def scatter(i, h):
                    tile = tiles(i, h)
                    pe.wait_ge(sums_done[h], i + 1)
                    nc.tensor.matmul(agg(h)[:, 0:1], m.zeros[:, 0:z.NT], m.ones[:, 0:1],
                                     start=True, stop=False, skip_group_check=True)
                    has_last = pe.value_load(m.last_chunk[:, bass.ds(tile, 1)], min_val=0, max_val=1)
                    with pe.Fori(0, groups) as g:
                        group = pe.snap(tile * groups + g)
                        pe.wait_ge(select_done[h], 2 * (i * groups + g) + 2)
                        for k in z.order(layer):
                            if k == LAST - 1:
                                with pe.If(has_last == 1):
                                    last_before = pe.value_load(m.last_before[:, bass.ds(tile, 1)], min_val=0,
                                                                max_val=z.TILES * z.ALL_GROUPS)
                                    pe.wait_ge(gathered[LAST], 16 * (last_before + g) + 16)
                                    nc.tensor.matmul(agg(h), select[h][:, LAST - SPLIT, :], rows[:, LAST, :], start=False,
                                                     stop=False, skip_group_check=True)
                            if k < SPLIT:
                                pe.wait_ge(split_lo, (group + 1) * SPLIT + k + 1)
                                nc.tensor.matmul(agg(h), select_r[h][:, k, :], rows_hi[:, k, :], start=False,
                                                 stop=False, skip_group_check=True)
                                last = nc.tensor.matmul(agg(h), select_r[h][:, k, :], rows_lo[:, k, :], start=False,
                                                        stop=False, skip_group_check=True)
                            else:
                                pe.wait_ge(gathered[k], 16 * group + 16)
                                last = nc.tensor.matmul(agg(h), select[h][:, k - SPLIT, :], rows[:, k, :], start=False,
                                                        stop=layer == 0 and k == LAST - 1, skip_group_check=True)
                            if k < SPLIT:
                                last.then_inc(split_used, 1)
                            if k >= SPLIT and (k + 1 in BLOCKS or k + 1 == LAST):
                                last.then_inc(slots_free, 1)
                        if layer == 0:
                            pe.wait_ge(counted[h], i * groups + g + 1)
                            for n in range(2):
                                last = nc.tensor.matmul(count_ps[0:z.NT, bass.ds(tile, 1)], edge_count[h][:, n, :],
                                                        m.ones[:, 0:1], start=False, stop=n == 1,
                                                        skip_group_check=True)
                        else:
                            last = nc.tensor.matmul(agg(h)[:, 0:1], m.zeros[:, 0:z.NT], m.ones[:, 0:1],
                                                    start=False, stop=True, skip_group_check=True)
                        last.then_inc(scattered[h], 1)

                def turn(i):
                    if layer == 1:
                        pe.wait_ge(weights_lo, 1)
                    pe.wait_ge(lo_done, 2 * i + 1)
                    for h in range(2):
                        pe.wait_ge(sums_done[h], i + 2)
                    for k in range(z.KD):
                        for h in range(2):
                            at = (k % (z.KD // 2)) * z.W + h * z.NT
                            last = nc.tensor.transpose(turn_ps[:, k // (z.KD // 2), at:at + z.NT],
                                                       sums[h][:, k * P:(k + 1) * P], m.ident[0:z.NT, 0:z.NT])
                    last.then_inc(turned, 1)

                def product(i):
                    pe.wait_ge(lo_done, 2 * i + 3)
                    pe.wait_ge(weights_lo, 1)
                    for b in range(HALVES):
                        pe.wait_ge(product_out, HALVES * i + b + 1)
                        for o in (2 * b, 2 * b + 1):
                            out = prod_ps[:, b % 2, (o % 2) * z.W:(o % 2 + 1) * z.W]
                            parts = [(w, s, k) for k in range(z.KD)
                                     for w, s in ((w_hi, sumsT_hi), (w_hi, sumsT_lo), (w_lo, sumsT_hi))]
                            for n, (w, s, k) in enumerate(parts):
                                last = nc.tensor.matmul(out, w[:, k, o * P:(o + 1) * P], s[:, k, :], start=n == 0,
                                                        stop=n == len(parts) - 1)
                        last.then_inc(product_done, 1)

                if layer == 1:
                    pe.wait_ge(weights_in[0], 16 * z.KD)
                    for k in range(z.KD):
                        for o in range(z.KD):
                            last = nc.tensor.transpose(m.bank(2 + k)[:, o * P:(o + 1) * P],
                                                       weight_in[:, o * z.D + k * P:o * z.D + (k + 1) * P], m.ident[:])
                    last.then_inc(weight_turned, 1)
                if layer == 0:
                    nc.tensor.matmul(count_ps[0:z.NT, 0:z.TILES], m.zeros[:, 0:z.NT], m.ones[:],
                                     start=True, stop=False, skip_group_check=True)
                scatter(0, 0)
                scatter(0, 1)
                with pe.Fori(1, z.PAIRS) as i:
                    scatter(i, 0)
                    turn(i - 1)
                    scatter(i, 1)
                    product(i - 1)
                turn(z.PAIRS - 1)
                product(z.PAIRS - 1)

            @block.scalar
            def _(act):
                nc.scalar.sem_inc(product_out, 2)
                if layer == 0:
                    nc.scalar.sem_inc(m.hidden_stored, 16)
                groups = act.value_load(m.groups, min_val=1, max_val=z.ALL_GROUPS)

                def load_weight(n, k):
                    width = weight_d[n].shape[1]
                    act.dma_start(weight_in[:, k * width:(k + 1) * width], weight_d[n][k * P:(k + 1) * P, :]
                                  ).then_inc(weights_in[n], 16)

                FIRST_BANKS, LAST_BANKS = range(HALVES // 2), range(HALVES // 2, HALVES)

                def high_part(i):
                    act.wait_ge(turned, i + 2)
                    act.wait_ge(product_done, HALVES * i + 1)
                    for b in range(2):
                        nc.scalar.activation(
                            sumsT_hi[:, b * z.KD // 2:(b + 1) * z.KD // 2, :],
                            turn_ps[:, b, 0:z.W * z.KD // 2].rearrange("p (k n) -> p k n", n=z.W),
                            ACT.Copy).then_inc(hi_done, 1)

                def split(i, h):
                    with act.Fori(0, groups) as g:
                        split_rows(act.snap(tiles(i, h) * groups + g), range(SPLIT))

                def weight(n):
                    if layer == 0:
                        act.wait_ge(weights_in[n], 16 * (weight_d[n].shape[0] // P))
                        from_ = weight_in[:]
                    else:
                        act.wait_ge(weight_turned, 1)
                        from_ = flat(w3_ps)
                    nc.scalar.activation(flat(weight_hi[n]), from_, ACT.Copy).then_inc(weights_hi, 1)

                def split_rows(group, chunks):
                    for k in chunks:
                        act.wait_ge(split_used, SPLIT * group + k + 1)
                        act.wait_ge(gathered[k], 16 * group + 16)
                        nc.scalar.activation(rows_hi[:, k, :], rows[:, k, :], ACT.Copy).then_inc(split_hi, 1)

                def read_product(i, banks):
                    if layer == 0 and 0 in banks:
                        act.wait_ge(m.hidden_stored, 16 * i + 16)
                        act.wait_ge(stats_done, i + 1)
                    for b in banks:
                        act.wait_ge(product_done, HALVES * i + b + 2)
                        for o in (2 * b, 2 * b + 1):
                            from_ = prod_ps[:, b % 2, (o % 2) * z.W:(o % 2 + 1) * z.W]
                            if layer == 0:
                                nc.scalar.activation(hidden[:, o, :], from_, ACT.Identity,
                                                     bias=m.b1[:, o:o + 1]).then_inc(out_done, 1)
                            else:
                                nc.scalar.activation(m.h3T[:, o, bass.ds(i * z.W, z.W)], from_, ACT.Relu,
                                                     bias=m.b3[:, o:o + 1]).then_inc(out_done, 1)
                        act.wait_ge(out_done, KM * i + 2 * b + 2)
                        nc.scalar.sem_inc(product_out, 1)
                    if layer == 0 and HALVES - 1 in banks:
                        act.dma_start(m.hidden_d[bass.ds(i * P, P), :], hidden[:].rearrange("p k n -> p (k n)")
                                      ).then_inc(m.hidden_stored, 16)

                for k in range(z.KD):
                    if layer == 0:
                        act.wait_ge(gathered[k], 16)
                    load_weight(0, k)
                if layer == 1:
                    weight(0)
                split(0, 0)
                if layer == 0:
                    weight(0)
                split(0, 1)
                split(1, 0)
                with act.Fori(1, z.PAIRS - 1) as i:
                    split(i, 1)
                    high_part(i - 1)
                    read_product(i - 1, FIRST_BANKS)
                    split(i + 1, 0)
                    read_product(i - 1, LAST_BANKS)
                if layer == 0:
                    act.wait_ge(weights_lo, 1)
                    for k in range(z.KH):
                        load_weight(1, k)
                split(z.PAIRS - 1, 1)
                high_part(z.PAIRS - 2)
                if layer == 0:
                    weight(1)
                read_product(z.PAIRS - 2, range(HALVES))
                high_part(z.PAIRS - 1)
                read_product(z.PAIRS - 1, range(HALVES))


def batch_norm_constants(nc, z, m, dve_sem, act_sem, dve, act, stats, gamma, beta, scale, bias, blocks, tmp):
    if dve is not None:
        for k in range(blocks):
            last = nc.vector.bn_aggr(tmp[:, k, 0:2], stats[:, k, :])
        last.then_inc(dve_sem, 1)
        dve.wait_ge(act_sem, 1)
        nc.vector.reciprocal(scale[:], tmp[:, :, 2]).then_inc(dve_sem, 1)
        dve.wait_ge(dve_sem, 2)
        nc.vector.tensor_tensor(scale[:], scale[:], gamma[:], ALU.mult).then_inc(dve_sem, 1)
        dve.wait_ge(dve_sem, 3)
        nc.vector.tensor_tensor(bias[:], tmp[:, :, 0], scale[:], ALU.mult).then_inc(dve_sem, 1)
        dve.wait_ge(dve_sem, 4)
        nc.vector.tensor_tensor(bias[:], beta[:], bias[:], ALU.subtract).then_inc(dve_sem, 1)
    if act is not None:
        act.wait_ge(dve_sem, 1)
        nc.scalar.activation(tmp[:, :, 2], tmp[:, :, 1], ACT.Sqrt, bias=m.bn_eps[:, 0:1]).then_inc(act_sem, 1)
        act.wait_ge(dve_sem, 5)


def hidden_phase(nc, z, m):
    with ExitStack() as ctx:
        sb = lambda name, shape, dt=F32: ctx.enter_context(nc.sbuf_tensor(name, shape, dt))
        sem = PhaseSemaphores(nc, ctx, "hidden")
        two = lambda name: [sem(f"{name}{q}") for q in range(2)]
        act_f = [sb(f"act_f{q}", [P, z.KH, z.W]) for q in range(2)]
        act_hi = [sb(f"act_hi{q}", [P, z.KH, z.W], F32R) for q in range(2)]
        act_lo = [sb(f"act_lo{q}", [P, z.KH, z.W], F32R) for q in range(2)]
        scale, bias = sb("scale1", [P, z.KH]), sb("bias1", [P, z.KH])
        tmp = sb("bn_tmp1", [P, z.KH, 3])

        loaded = [two(f"loaded_{part}_") for part in "ab"]
        rectified = two("rectified")
        hi_done = two("hi_done")
        lo_done = two("lo_done")
        product_done = two("product_done")
        out_done = two("out_done")
        product_out = two("product_out")
        bn_dve, bn_act = sem("bn_dve"), sem("bn_act")

        HALVES = (slice(0, z.KH // 2), slice(z.KH // 2, z.KH))

        def out_ps(q, o):
            return m.bank(2 * q + o // 2)[:, (o % 2) * z.W:(o % 2 + 1) * z.W]

        def in_pairs(engine, first, steady, last):
            first()
            with engine.Fori(0, z.PAIRS // 2) as i:
                steady(2 * i, i, i, 0)
                steady(2 * i + 1, i, i + 1, 1)
            last()

        with nc.Block(name="hidden") as block:

            @block.sync
            def _(sp):
                def load(v, u, q):
                    for f, half in enumerate(HALVES):
                        sp.wait_ge(lo_done[q], 2 * u + f + 1)
                        sp.dma_start(act_f[q][:, half, :].rearrange("p k n -> p (k n)"),
                                     m.hidden_d[bass.ds(v * P, P), half.start * z.W:half.stop * z.W]
                                     ).then_inc(loaded[f][q], 16)

                with sp.Fori(0, z.PAIRS // 2) as i:
                    load(2 * i, i, 0)
                    load(2 * i + 1, i, 1)
                sp.wait_ge(m.hidden_stored, 16 * z.PAIRS + 16)
                load(z.PAIRS - 1, z.PAIRS // 2, 0)

            @block.scalar
            def _(act):
                for q in range(2):
                    nc.scalar.sem_inc(product_out[q], 1)
                batch_norm_constants(nc, z, m, bn_dve, bn_act, None, act, m.stats1, m.g1, m.be1, scale, bias, z.KH, tmp)

                def prepare(u, q):
                    for f, half in enumerate(HALVES):
                        act.wait_ge(loaded[f][q], 16 * u + 16)
                        for k in range(half.start, half.stop):
                            last = nc.scalar.activation(act_f[q][:, k, :], act_f[q][:, k, :], ACT.Relu,
                                                        scale=scale[:, k:k + 1], bias=bias[:, k:k + 1])
                        last.then_inc(rectified[q], 1)
                        act.wait_ge(rectified[q], 2 * u + f + 1)
                        act.wait_ge(product_done[q], u + 1)
                        nc.scalar.activation(act_hi[q][:, half, :], act_f[q][:, half, :], ACT.Copy
                                             ).then_inc(hi_done[q], 1)

                def read_out(v, u, q):
                    act.wait_ge(product_done[q], u + 2)
                    for o in range(z.KD):
                        nc.scalar.activation(m.h2T[:, o, bass.ds(v * z.W, z.W)], out_ps(q, o), ACT.Identity,
                                             bias=m.b2[:, o:o + 1]).then_inc(out_done[q], 1)
                    act.wait_ge(out_done[q], z.KD * u + z.KD)
                    nc.scalar.sem_inc(product_out[q], 1)

                def steady(v, u, next_u, q):
                    prepare(next_u if q == 0 else next_u, 1 - q)
                    read_out(v, u, q)

                def first():
                    prepare(0, 0)
                    act.wait_ge(m.hidden_stored, 16 * z.PAIRS + 16)

                in_pairs(act, first, steady,
                         lambda: read_out(z.PAIRS - 1, z.PAIRS // 2, 0))

            @block.vector
            def _(dve):
                for q in range(2):
                    nc.vector.sem_inc(lo_done[q], 2)
                batch_norm_constants(nc, z, m, bn_dve, bn_act, dve, None, m.stats1, m.g1, m.be1, scale, bias, z.KH, tmp)

                def low_part(u, q):
                    for f, half in enumerate(HALVES):
                        dve.wait_ge(hi_done[q], 2 * u + f + 1)
                        nc.vector.tensor_tensor(act_lo[q][:, half, :], act_f[q][:, half, :],
                                                act_hi[q][:, half, :].bitcast(F32), ALU.subtract
                                                ).then_inc(lo_done[q], 1)

                def statistics(v, u, q):
                    for o in range(z.KD):
                        dve.wait_ge(out_done[q], z.KD * u + o + 1)
                        nc.vector.bn_stats(m.stats2[:, o, bass.ds(v * 6, 6)], m.h2T[:, o, bass.ds(v * z.W, z.W)])

                def steady(v, u, next_u, q):
                    low_part(next_u, 1 - q)
                    statistics(v, u, q)

                in_pairs(dve, lambda: low_part(0, 0), steady,
                         lambda: statistics(z.PAIRS - 1, z.PAIRS // 2, 0))

            @block.tensor
            def _(pe):
                for q in range(2):
                    nc.tensor.sem_inc(product_done[q], 1)

                def product(u, q):
                    pe.wait_ge(lo_done[q], 2 * u + 4)
                    pe.wait_ge(product_out[q], u + 1)
                    for o in range(z.KD):
                        parts = [(w, s, k) for k in range(z.KH) for w, s in (
                            (m.w2_hi, act_hi[q]), (m.w2_hi, act_lo[q]), (m.w2_lo, act_hi[q]))]
                        for n, (w, s, k) in enumerate(parts):
                            last = nc.tensor.matmul(out_ps(q, o), w[:, k, o * P:(o + 1) * P], s[:, k, :],
                                                    start=n == 0, stop=n == len(parts) - 1)
                    last.then_inc(product_done[q], 1)

                with pe.Fori(0, z.PAIRS // 2) as i:
                    product(i, 0)
                    product(i, 1)
                product(z.PAIRS // 2, 0)


def rows_phase(nc, z, m, layer):
    featT, stats = (m.h2T, m.stats2) if layer == 0 else (m.h3T, m.stats3)
    gamma, beta = (m.g2, m.be2) if layer == 0 else (m.g3, m.be3)
    table, out_d = (m.x_d, m.x1_d) if layer == 0 else (m.x1_d, m.out_d)
    times = 2.0 if layer == 0 else 1.0
    U = z.STEP_TILES
    STEPS = z.TILES // U
    SW = U * z.NT
    PARTS = 16 * len(sprayed(z.NT))
    N_ACT = U - 1
    assert STEPS % 2 == 0 and STEPS >= 6
    with ExitStack() as ctx:
        sb = lambda name, shape, dt=F32: ctx.enter_context(nc.sbuf_tensor(f"{name}_r{layer}", shape, dt))
        sem = PhaseSemaphores(nc, ctx, f"rows{layer}")
        two = lambda name: [sem(f"{name}{b}") for b in range(2)]
        normed = sb("normed", [P, z.KD, SW])
        own = [sb(f"own{b}", [z.NT, U, z.D]) for b in range(2)]
        y = [sb(f"y{b}", [z.NT, U, z.D]) for b in range(2)]
        done = [sb(f"done{b}", [z.NT, U, z.D]) for b in range(2)]
        six = sb("six", [z.NT, U, 6])
        mean_var = [sb(f"mean_var{b}", [z.NT, U, 2]) for b in range(2)]
        deviation = sb("deviation", [z.NT, U])
        inverse = sb("inverse", [z.NT, U])
        offset = sb("offset", [z.NT, U])
        scale, bias = sb("scale", [P, z.KD]), sb("bias", [P, z.KD])
        tmp = sb("bn_tmp", [P, z.KD, 3])

        own_in = two("own_in")
        normed_done = sem("normed_done")
        turned = sem("turned")
        y_done = sem("y_done")
        six_done = sem("six_done")
        aggr_done = sem("aggr_done")
        deviation_done, inverse_done, offset_done = sem("deviation_done"), sem("inverse_done"), sem("offset_done")
        norm_done = sem("norm_done")
        norm_pool = sem("norm_pool")
        stored = two("stored")
        waited = sem("waited")
        bn_dve, bn_act = sem("bn_dve"), sem("bn_act")

        def rows_of(dram, i):
            return dram[bass.ds(i * SW, SW), :].rearrange("(u p) d -> p u d", u=U)

        with nc.Block(name=f"rows{layer}") as block:

            @block.sync
            def _(sp):
                def load(i, b):
                    for p, q in sprayed(z.NT):
                        sp.dma_start(own[b][p:q, :, :], rows_of(table, i)[p:q, :, :]).then_inc(own_in[b], 16)

                def store(i, b, tiles=slice(0, U)):
                    if tiles.stop == U:
                        sp.wait_ge(norm_done, N_ACT * (i + 1))
                        sp.wait_ge(norm_pool, i + 1)
                    else:
                        sp.wait_ge(norm_done, N_ACT * i + tiles.stop)
                    for p, q in sprayed(z.NT):
                        sp.dma_start(rows_of(out_d, i)[p:q, tiles, :], done[b][p:q, tiles, :]).then_inc(stored[b], 16)

                def reload(i, b):
                    sp.wait_ge(y_done, U * i)
                    load(i, b)

                load(0, 0)
                load(1, 1)
                reload(2, 0)
                with sp.Fori(1, STEPS // 2 - 1) as j:
                    for b in range(2):
                        i = 2 * j + 1 + b
                        reload(i, 1 - b)
                        store(i - 3, b)
                reload(STEPS - 1, 1)
                for i in range(STEPS - 4, STEPS - 1):
                    store(i, i % 2)
                store(STEPS - 1, 1, slice(0, U // 2))
                store(STEPS - 1, 1, slice(U // 2, U))
                sp.wait_ge(stored[0], PARTS * (STEPS // 2))
                sp.wait_ge(stored[1], PARTS * (STEPS // 2 + 1))

            @block.scalar
            def _(act):
                batch_norm_constants(nc, z, m, bn_dve, bn_act, None, act, stats, gamma, beta, scale, bias, z.KD, tmp)

                def features(i):
                    for k in range(z.KD):
                        last = nc.scalar.activation(normed[:, k, :], featT[:, k, bass.ds(i * SW, SW)],
                                                    ACT.Relu if layer == 0 else ACT.Identity,
                                                    scale=scale[:, k:k + 1], bias=bias[:, k:k + 1])
                    last.then_inc(normed_done, 1)

                def deviations(i, b):
                    act.wait_ge(aggr_done, i + 1)
                    nc.scalar.activation(deviation[:], mean_var[b][:, :, 1], ACT.Sqrt,
                                         bias=m.ln_eps[0:z.NT, 0:1]).then_inc(deviation_done, 1)

                def rows(i, b):
                    act.wait_ge(offset_done, i + 1)
                    for u in range(N_ACT):
                        nc.scalar.activation(done[b][:, u, :], y[b][:, u, :], ACT.Identity,
                                             scale=inverse[:, u:u + 1], bias=offset[:, u:u + 1]).then_inc(norm_done, 1)

                features(0)
                act.wait_ge(turned, U)
                features(1)

                def steady(i, j, b, first):
                    deviations(i - 2, b)
                    act.wait_ge(turned, U * i)
                    features(i)
                    if not first:
                        act.wait_ge(stored[b], PARTS * (j - 1))
                    rows(i - 2, b)

                for b in range(2):
                    steady(2 + b, 1, b, True)
                with act.Fori(2, STEPS // 2) as j:
                    for b in range(2):
                        steady(2 * j + b, j, b, False)
                for b in range(2):
                    i = STEPS - 2 + b
                    deviations(i, b)
                    act.wait_ge(stored[b], PARTS * (STEPS // 2 - 1))
                    rows(i, b)

            @block.gpsimd
            def _(pool):
                def rows(i, b, reuse):
                    pool.wait_ge(offset_done, i + 1)
                    if reuse is not None:
                        pool.wait_ge(stored[b], PARTS * reuse)
                    nc.gpsimd.sem_inc(waited, 1)
                    for u in range(N_ACT, U):
                        last = nc.gpsimd.tensor_scalar(done[b][:, u, :], y[b][:, u, :], inverse[:, u:u + 1],
                                                       offset[:, u:u + 1], ALU.mult, ALU.add)
                    last.then_inc(norm_pool, 1)

                rows(0, 0, None)
                rows(1, 1, None)
                with pool.Fori(1, STEPS // 2) as j:
                    for b in range(2):
                        rows(2 * j + b, b, j)

            @block.tensor
            def _(pe):
                def turn(i):
                    pe.wait_ge(normed_done, i + 1)
                    for u in range(U):
                        pe.wait_ge(y_done, U * i + u + 1)
                        for k in range(z.KD):
                            last = nc.tensor.transpose(m.bank(u)[0:z.NT, k * P:(k + 1) * P],
                                                       normed[:, k, u * z.NT:(u + 1) * z.NT], m.ident[:])
                        last.then_inc(turned, 1)

                turn(0)
                with pe.Fori(1, STEPS) as i:
                    turn(i)

            @block.vector
            def _(dve):
                nc.vector.sem_inc(y_done, U)
                batch_norm_constants(nc, z, m, bn_dve, bn_act, dve, None, stats, gamma, beta, scale, bias, z.KD, tmp)

                def inverses(i, b, first):
                    dve.wait_ge(deviation_done, i + 1)
                    if not first:
                        dve.wait_ge(norm_pool, i)
                    nc.vector.reciprocal(inverse[:], deviation[:]).then_inc(inverse_done, 1)
                    dve.wait_ge(inverse_done, i + 1)
                    nc.vector.scalar_tensor_tensor(offset[:], mean_var[b][:, :, 0], -1.0, inverse[:], ALU.mult,
                                                   ALU.mult).then_inc(offset_done, 1)

                def sums(i, b, u):
                    dve.wait_ge(turned, U * i + u + 1)
                    nc.vector.scalar_tensor_tensor(y[b][:, u, :], own[b][:, u, :], times, m.bank(u)[0:z.NT, 0:z.D],
                                                   ALU.mult, ALU.add).then_inc(y_done, 1)

                def moments(i, b, u):
                    dve.wait_ge(y_done, U * (i + 1) + u + 1)
                    nc.vector.bn_stats(six[:, u, :], y[b][:, u, :]).then_inc(six_done, 1)

                def mean_variance(i, b, u):
                    dve.wait_ge(six_done, U * i + u + 1)
                    nc.vector.sem_inc(waited, 1)
                    last = nc.vector.bn_aggr(mean_var[b][:, u, :], six[:, u, :])
                    if u == U - 1:
                        last.then_inc(aggr_done, 1)

                def step(i, j, b, first, second):
                    dve.wait_ge(own_in[b], PARTS * (j + 1))
                    for n in range(U + 2):
                        if n == 2 and not first:
                            inverses(i - 1, 1 - b, second)
                        if n < U:
                            sums(i, b, n)
                        if 0 <= n - 2:
                            mean_variance(i, b, n - 2)
                        if 0 <= n - 1 < U:
                            moments(i, b, n - 1)

                step(0, 0, 0, True, False)
                step(1, 0, 1, False, True)
                with dve.Fori(1, STEPS // 2) as j:
                    for b in range(2):
                        dve.wait_ge(norm_done, N_ACT * (2 * j + b - 1))
                        dve.wait_ge(norm_pool, 2 * j + b - 1)
                        step(2 * j + b, j, b, False, False)
                inverses(STEPS - 1, 1, False)


class Memory:
    pass


def gnn_kernel(nc, x, src, dst, eps, w1, b1, g1, be1, w2, b2, g2, be2, w3, b3, g3, be3, out):
    z = Shapes(x.shape[0], x.shape[1], src.shape[0], w1.shape[1])
    m = Memory()
    m.x_d, m.src_d, m.dst_d, m.eps_d, m.w1_d, m.w2_d, m.w3_d, m.out_d = x, src, dst, eps, w1, w2, w3, out
    m.b1_d, m.g1_d, m.be1_d, m.b2_d, m.g2_d, m.be2_d, m.b3_d, m.g3_d, m.be3_d = b1, g1, be1, b2, g2, be2, b3, g3, be3
    m.src_pad = nc.dram_tensor("src_pad", (z.E + z.GROUP,), I32, kind="Internal").ap()
    m.dst_pad = nc.dram_tensor("dst_pad", (z.E + z.GROUP,), I32, kind="Internal").ap()
    m.hidden_d = nc.dram_tensor("hidden_d", (z.PAIRS * P, z.KH * z.W), F32, kind="Internal").ap()
    m.x1_d = nc.dram_tensor("x1_d", (z.N, z.D), F32, kind="Internal").ap()
    with ExitStack() as ctx:
        def sb(name, shape, dt=F32, side="left", scope=ctx):
            return scope.enter_context(nc.sbuf_tensor(name, shape, dt, side=side))

        psum = ctx.enter_context(nc.psum_tensor("psum", [P, 8, 512], F32))
        m.hidden_stored = nc.alloc_semaphore("hidden_stored")
        m.bank = lambda b: psum[:, b, :]
        m.banks = lambda a, b: psum[:, a:b, :]
        m.column_ps = psum[:, 6, 0:z.NT]
        m.column, m.ident = sb("column", [P, P]), sb("ident", [P, P])
        m.self_weight, m.zeros, m.ones = sb("self_weight", [P, 1]), sb("zeros", [P, P], BF16), sb("ones", [P, z.TILES], BF16)
        m.tile_base, m.lone = sb("tile_base", [P, z.TILES]), sb("lone", [z.NT, z.TILES])
        control = sb("control", [1, 3 * z.TILES + 1], I32)
        m.starts, m.last_chunk, m.last_before = (control[:, n * z.TILES:(n + 1) * z.TILES] for n in range(3))
        m.groups = control[:, 3 * z.TILES:]
        m.bn_eps, m.ln_eps = sb("bn_eps", [P, 1]), sb("ln_eps", [P, 1])
        m.b1, m.g1, m.be1 = (sb(n, [P, z.KH]) for n in ("b1", "g1", "be1"))
        m.b2, m.g2, m.be2, m.b3, m.g3, m.be3 = (sb(n, [P, z.KD]) for n in ("b2", "g2", "be2", "b3", "g3", "be3"))
        m.stats1 = sb("stats1", [P, z.KH, z.PAIRS * 6])
        m.stats2 = sb("stats2", [P, z.KD, z.PAIRS * 6])
        m.stats3 = sb("stats3", [P, z.KD, z.PAIRS * 6])

        with ExitStack() as second:
            m.w2_hi = sb("w2_hi", [P, z.KH, z.D], F32R, scope=second)
            m.w2_lo = sb("w2_lo", [P, z.KH, z.D], F32R, scope=second)
            with ExitStack() as first:
                m.w1_hi = sb("w1_hi", [P, z.KD, z.H], F32R, scope=first)
                m.w1_lo = sb("w1_lo", [P, z.KD, z.H], F32R, scope=first)
                setup_phase(nc, z, m)
                gather_phase(nc, z, m, 0)
            features = ExitStack()
            m.h2T = sb("h2T", [P, z.KD, z.N], side="right", scope=features)
            hidden_phase(nc, z, m)
        rows_phase(nc, z, m, 0)
        features.close()
        m.w3_hi, m.w3_lo = sb("w3_hi", [P, z.KD, z.D], F32R), sb("w3_lo", [P, z.KD, z.D], F32R)
        m.h3T = sb("h3T", [P, z.KD, z.N], side="right")
        gather_phase(nc, z, m, 1)
        rows_phase(nc, z, m, 1)


_INS = ["x", "src", "dst", "L0_gnn_eps", "L0_gnn_W1", "L0_gnn_b1", "L0_gnn_g1", "L0_gnn_be1", "L0_gnn_W2",
        "L0_gnn_b2", "L0_gnn_g2", "L0_gnn_be2", "L1_gnn_W", "L1_gnn_b", "L1_gnn_gamma", "L1_gnn_beta"]


def kernel(**inputs):
    import numpy as np
    import concourse.bacc as bacc
    from concourse.bass_utils import run_bass_kernel_spmd

    nc = bacc.Bacc("TRN2", target_bir_lowering=False, num_devices=1)
    arrays, args = {}, []
    for name in _INS:
        a = np.asarray(inputs[name])
        a = np.ascontiguousarray(a.reshape((1,)) if a.ndim == 0 else a)
        arrays[f"{name}_in"] = a
        args.append(nc.dram_tensor(f"{name}_in", a.shape, mybir.dt.from_np(a.dtype), kind="ExternalInput").ap())
    args.append(nc.dram_tensor("rows_out", arrays["x_in"].shape, F32, kind="ExternalOutput").ap())
    gnn_kernel(nc, *args)
    return run_bass_kernel_spmd(nc, [arrays], core_ids=[0]).results[0]["rows_out"]
```
